# Optimizing a Trainium2 kernel written in Bass

```python
import numpy as np
import jax
import jax.numpy as jnp

def _softmax(x, axis=-1):
    return jax.nn.softmax(x, axis=axis)

def _gelu(x):
    return jax.nn.gelu(x, approximate=True)

def _silu(x):
    return jax.nn.silu(x)

def _sigmoid(x):
    return jax.nn.sigmoid(x)

def _layernorm(x, axis=-1, eps=1e-05):
    m = jnp.mean(x, axis=axis, keepdims=True)
    v = jnp.var(x, axis=axis, keepdims=True)
    return (x - m) / jnp.sqrt(v + eps)

def _scatter_add(tgt, idx, src, axis=0):
    return tgt.at[idx].add(src)

def _segment_sum(src, seg, n):
    return jax.ops.segment_sum(src, seg, n)
kernel_name = 'mk_perceiver_d2_seqx_r2_59c0d2'

def setup_inputs(seed: int=0):
    np.random.seed(seed)
    _w = jnp.asarray

    def _rec_inputs():
        import jax
        import jax.numpy as jnp
        _rk = jax.random.key(seed)
        x = -0.0002928 + 1 * jax.random.normal(jax.random.fold_in(_rk, 1), (8, 128, 512), jnp.float32)
        _lenS = 128 - jax.random.randint(jax.random.fold_in(_rk, 7), (8,), 0, max(1, 128 // 4) + 1, jnp.int32)
        _lenS2 = 2048 - jax.random.randint(jax.random.fold_in(_rk, 8), (8,), 0, max(1, 2048 // 4) + 1, jnp.int32)
        _ctx_1024P = jax.random.normal(jax.random.fold_in(_rk, 11), (8, 16, 512), jnp.float32)
        _ctx_1024c = jax.random.dirichlet(jax.random.fold_in(_rk, 511), 0.3 * jnp.ones((16,), jnp.float32), (8, 2048))
        _ctx_1024t = jnp.einsum('bsk,bkd->bsd', _ctx_1024c, _ctx_1024P)
        _ctx_1024t = _ctx_1024t * jax.lax.rsqrt(jnp.mean(jnp.square(_ctx_1024t)) + 1e-12) * 0.953939
        ctx_1024 = -1.39393e-06 + 0.999914 * (_ctx_1024t + 0.3 * jax.random.normal(jax.random.fold_in(_rk, 611), (8, 2048, 512), jnp.float32))
        return (x, ctx_1024)
    x, ctx_1024 = _rec_inputs()

    def _L0_xattn_setup():
        import jax, jax.numpy as jnp
        import numpy as np
        NOT_EPSILON = 1.0
        W_SCALE = 0.05
        H, T, A, C = (8, 512, 64, 128)

        def swishmax(x, axis):
            m = jnp.max(x, axis=axis, keepdims=True)
            xe = x * jnp.exp(x - m)
            return xe / (jnp.sum(jnp.abs(xe), axis=axis, keepdims=True) + NOT_EPSILON)
        key = jax.random.key(seed)
        ks = jax.random.split(key, 7)
        B, Q, K = (2, 1024, 1024)
        return {'query_tokens': jax.random.normal(ks[0], (B, Q, T), dtype=jnp.float32), 'key_tokens': jax.random.normal(ks[1], (B, K, T), dtype=jnp.float32), 'key_down': jax.random.normal(ks[2], (H, T, A), dtype=jnp.float32) * W_SCALE, 'query_down': jax.random.normal(ks[3], (H, T, A), dtype=jnp.float32) * W_SCALE, 'query_down_bias': jax.random.normal(ks[4], (H, 1, A), dtype=jnp.float32) * W_SCALE, 'value_down': jax.random.normal(ks[5], (H, T, C), dtype=jnp.float32) * W_SCALE, 'value_up': jax.random.normal(ks[6], (H, C, T), dtype=jnp.float32) * W_SCALE}
    _L0_xattn_all = _L0_xattn_setup()
    _L0_xattn_in = {k: v for k, v in _L0_xattn_all.items() if k in ('key_down', 'query_down', 'query_down_bias', 'value_down', 'value_up')}
    del _L0_xattn_all

    def _L0_attn_setup():
        import jax, jax.numpy as jnp
        import numpy as np
        import math
        DIM = 512
        NUM_HEADS = 16
        HEAD_DIM = DIM // NUM_HEADS
        LAYER_IDX = 12
        LAMBDA_INIT = 0.8 - 0.6 * math.exp(-0.3 * (LAYER_IDX - 1))
        LN_EPS = 1e-05
        key = jax.random.key(seed)
        ks = jax.random.split(key, 11)
        B, S = (2, 1024)
        x = jax.random.normal(ks[0], (B, S, DIM), dtype=jnp.float32)
        s = 1.0 / math.sqrt(DIM)
        Wq = jax.random.normal(ks[1], (DIM, 2 * DIM), dtype=jnp.float32) * s
        Wk = jax.random.normal(ks[2], (DIM, 2 * DIM), dtype=jnp.float32) * s
        Wv = jax.random.normal(ks[3], (DIM, DIM), dtype=jnp.float32) * s
        Wo = jax.random.normal(ks[4], (DIM, DIM), dtype=jnp.float32) * s
        lambda_q1 = jax.random.normal(ks[5], (HEAD_DIM,), dtype=jnp.float32) * 0.1
        lambda_k1 = jax.random.normal(ks[6], (HEAD_DIM,), dtype=jnp.float32) * 0.1
        lambda_q2 = jax.random.normal(ks[7], (HEAD_DIM,), dtype=jnp.float32) * 0.1
        lambda_k2 = jax.random.normal(ks[8], (HEAD_DIM,), dtype=jnp.float32) * 0.1
        gamma = jnp.ones((DIM,), dtype=jnp.float32)
        beta = jnp.zeros((DIM,), dtype=jnp.float32)
        return {'x': x, 'Wq': Wq, 'Wk': Wk, 'Wv': Wv, 'Wo': Wo, 'lambda_q1': lambda_q1, 'lambda_k1': lambda_k1, 'lambda_q2': lambda_q2, 'lambda_k2': lambda_k2, 'gamma': gamma, 'beta': beta}
    _L0_attn_all = _L0_attn_setup()
    _L0_attn_in = {k: v for k, v in _L0_attn_all.items() if k in ('Wq', 'Wk', 'Wv', 'Wo', 'lambda_q1', 'lambda_k1', 'lambda_q2', 'lambda_k2', 'gamma', 'beta')}
    del _L0_attn_all

    def _L0_ffn_setup():
        import jax, jax.numpy as jnp
        import numpy as np
        D_MODEL = 512
        N_HEADS = 16
        N_EXPERTS = 8
        TOP_K = 2
        EXPERT_HIDDEN = D_MODEL * 4 // N_EXPERTS

        def layer_norm(x, g, b, eps=1e-05):
            mu = jnp.mean(x, axis=-1, keepdims=True)
            var = jnp.var(x, axis=-1, keepdims=True)
            return (x - mu) * jax.lax.rsqrt(var + eps) * g + b
        key = jax.random.key(seed)
        ks = jax.random.split(key, 12)
        s = 1.0 / np.sqrt(D_MODEL)
        return {'x': jax.random.normal(ks[0], (2, 1024, D_MODEL), dtype=jnp.float32), 'Wq': jax.random.normal(ks[1], (D_MODEL, D_MODEL), dtype=jnp.float32) * s, 'Wk': jax.random.normal(ks[2], (D_MODEL, D_MODEL), dtype=jnp.float32) * s, 'Wv': jax.random.normal(ks[3], (D_MODEL, D_MODEL), dtype=jnp.float32) * s, 'Wo': jax.random.normal(ks[4], (D_MODEL, D_MODEL), dtype=jnp.float32) * s, 'g1': jnp.ones((D_MODEL,), jnp.float32), 'b1': jnp.zeros((D_MODEL,), jnp.float32), 'g2': jnp.ones((D_MODEL,), jnp.float32), 'b2': jnp.zeros((D_MODEL,), jnp.float32), 'Wg': jax.random.normal(ks[5], (D_MODEL, N_EXPERTS), dtype=jnp.float32) * s, 'W1': jax.random.normal(ks[6], (N_EXPERTS, D_MODEL, EXPERT_HIDDEN), dtype=jnp.float32) * s, 'W2': jax.random.normal(ks[7], (N_EXPERTS, EXPERT_HIDDEN, D_MODEL), dtype=jnp.float32) * (1.0 / np.sqrt(EXPERT_HIDDEN))}
    _L0_ffn_all = _L0_ffn_setup()
    _L0_ffn_in = {k: v for k, v in _L0_ffn_all.items() if k in ('Wq', 'Wk', 'Wv', 'Wo', 'g1', 'b1', 'g2', 'b2', 'Wg', 'W1', 'W2')}
    del _L0_ffn_all

    def _L1_xattn_setup():
        import jax, jax.numpy as jnp
        import numpy as np
        D_MODEL = 512
        NUM_HEADS = 16
        HEAD_DIM = D_MODEL // NUM_HEADS
        key = jax.random.key(seed)
        ks = jax.random.split(key, 11)
        B, T, S = (2, 1024, 1024)
        s = 1.0 / np.sqrt(D_MODEL)
        return {'query': jax.random.normal(ks[0], (B, T, D_MODEL), jnp.float32), 'key': jax.random.normal(ks[1], (B, S, D_MODEL), jnp.float32), 'value': jax.random.normal(ks[2], (B, S, D_MODEL), jnp.float32), 'Wq': jax.random.normal(ks[3], (D_MODEL, D_MODEL), jnp.float32) * s, 'bq': jnp.zeros((D_MODEL,), jnp.float32), 'Wk': jax.random.normal(ks[4], (D_MODEL, D_MODEL), jnp.float32) * s, 'bk': jnp.zeros((D_MODEL,), jnp.float32), 'Wv': jax.random.normal(ks[5], (D_MODEL, D_MODEL), jnp.float32) * s, 'bv': jnp.zeros((D_MODEL,), jnp.float32), 'Wo': jax.random.normal(ks[6], (D_MODEL, D_MODEL), jnp.float32) * s, 'bo': jnp.zeros((D_MODEL,), jnp.float32)}
    _L1_xattn_all = _L1_xattn_setup()
    _L1_xattn_in = {k: v for k, v in _L1_xattn_all.items() if k in ('Wq', 'bq', 'Wk', 'bk', 'Wv', 'bv', 'Wo', 'bo')}
    del _L1_xattn_all

    def _L1_attn_setup():
        import jax, jax.numpy as jnp
        import numpy as np
        import math
        EPS = 1e-06

        def favorplus_features(x, proj):
            xw = jnp.einsum('bhtd,hmd->bhtm', x, proj)
            xw = xw - jnp.max(xw, axis=-1, keepdims=True)
            x_norm_sq = jnp.sum(x * x, axis=-1, keepdims=True)
            return jnp.exp(xw) * jnp.exp(-0.5 * x_norm_sq) + EPS
        key = jax.random.key(seed)
        ks = jax.random.split(key, 6)
        B, T, d = (2, 2048, 512)
        h, m = (16, 128)
        dk = d // h
        s = 1.0 / math.sqrt(d)
        return {'x': jax.random.normal(ks[0], (B, T, d), dtype=jnp.float32), 'Wq': jax.random.normal(ks[1], (d, d), dtype=jnp.float32) * s, 'Wk': jax.random.normal(ks[2], (d, d), dtype=jnp.float32) * s, 'Wv': jax.random.normal(ks[3], (d, d), dtype=jnp.float32) * s, 'Wo': jax.random.normal(ks[4], (d, d), dtype=jnp.float32) * s, 'bo': jnp.zeros((d,), dtype=jnp.float32), 'proj': jax.random.normal(ks[5], (h, m, dk), dtype=jnp.float32)}
    _L1_attn_all = _L1_attn_setup()
    _L1_attn_in = {k: v for k, v in _L1_attn_all.items() if k in ('Wq', 'Wk', 'Wv', 'Wo', 'bo', 'proj')}
    del _L1_attn_all

    def _L1_ffn_setup():
        import jax, jax.numpy as jnp
        import numpy as np
        D_MODEL = 512
        M = 64
        INNER = 16
        key = jax.random.key(seed)
        ks = jax.random.split(key, 9)

        def init(k, shape, fan_in):
            bound = 1.0 / np.sqrt(fan_in)
            return jax.random.uniform(k, shape, jnp.float32, -bound, bound)
        x = jax.random.normal(ks[0], (16, 2048, D_MODEL), dtype=jnp.float32)
        Win = init(ks[1], (D_MODEL, M), D_MODEL)
        bin_ = init(ks[2], (M,), D_MODEL)
        W1 = init(ks[3], (M, INNER), 1)
        b1 = init(ks[4], (M, INNER), 1)
        W2 = init(ks[5], (M, INNER), INNER)
        b2 = init(ks[6], (M,), INNER)
        Wout = init(ks[7], (M, D_MODEL), M)
        bout = init(ks[8], (D_MODEL,), M)
        return {'x': x, 'Win': Win, 'bin_': bin_, 'W1': W1, 'b1': b1, 'W2': W2, 'b2': b2, 'Wout': Wout, 'bout': bout}
    _L1_ffn_all = _L1_ffn_setup()
    _L1_ffn_in = {k: v for k, v in _L1_ffn_all.items() if k in ('Win', 'bin_', 'W1', 'b1', 'W2', 'b2', 'Wout', 'bout')}
    del _L1_ffn_all
    return {'x': x, 'ctx_1024': ctx_1024, 'L0_xattn_key_down': _L0_xattn_in['key_down'], 'L0_xattn_query_down': _L0_xattn_in['query_down'], 'L0_xattn_query_down_bias': _L0_xattn_in['query_down_bias'], 'L0_xattn_value_down': _L0_xattn_in['value_down'], 'L0_xattn_value_up': _L0_xattn_in['value_up'], 'L0_attn_Wq': _L0_attn_in['Wq'], 'L0_attn_Wk': _L0_attn_in['Wk'], 'L0_attn_Wv': _L0_attn_in['Wv'], 'L0_attn_Wo': _L0_attn_in['Wo'], 'L0_attn_lambda_q1': _L0_attn_in['lambda_q1'], 'L0_attn_lambda_k1': _L0_attn_in['lambda_k1'], 'L0_attn_lambda_q2': _L0_attn_in['lambda_q2'], 'L0_attn_lambda_k2': _L0_attn_in['lambda_k2'], 'L0_attn_gamma': _L0_attn_in['gamma'], 'L0_attn_beta': _L0_attn_in['beta'], 'L0_ffn_Wq': _L0_ffn_in['Wq'], 'L0_ffn_Wk': _L0_ffn_in['Wk'], 'L0_ffn_Wv': _L0_ffn_in['Wv'], 'L0_ffn_Wo': _L0_ffn_in['Wo'], 'L0_ffn_g1': _L0_ffn_in['g1'], 'L0_ffn_b1': _L0_ffn_in['b1'], 'L0_ffn_g2': _L0_ffn_in['g2'], 'L0_ffn_b2': _L0_ffn_in['b2'], 'L0_ffn_Wg': _L0_ffn_in['Wg'], 'L0_ffn_W1': _L0_ffn_in['W1'], 'L0_ffn_W2': _L0_ffn_in['W2'], 'L1_xattn_Wq': _L1_xattn_in['Wq'], 'L1_xattn_bq': _L1_xattn_in['bq'], 'L1_xattn_Wk': _L1_xattn_in['Wk'], 'L1_xattn_bk': _L1_xattn_in['bk'], 'L1_xattn_Wv': _L1_xattn_in['Wv'], 'L1_xattn_bv': _L1_xattn_in['bv'], 'L1_xattn_Wo': _L1_xattn_in['Wo'], 'L1_xattn_bo': _L1_xattn_in['bo'], 'L1_attn_Wq': _L1_attn_in['Wq'], 'L1_attn_Wk': _L1_attn_in['Wk'], 'L1_attn_Wv': _L1_attn_in['Wv'], 'L1_attn_Wo': _L1_attn_in['Wo'], 'L1_attn_bo': _L1_attn_in['bo'], 'L1_attn_proj': _L1_attn_in['proj'], 'L1_ffn_Win': _L1_ffn_in['Win'], 'L1_ffn_bin_': _L1_ffn_in['bin_'], 'L1_ffn_W1': _L1_ffn_in['W1'], 'L1_ffn_b1': _L1_ffn_in['b1'], 'L1_ffn_W2': _L1_ffn_in['W2'], 'L1_ffn_b2': _L1_ffn_in['b2'], 'L1_ffn_Wout': _L1_ffn_in['Wout'], 'L1_ffn_bout': _L1_ffn_in['bout']}

def reference(x, ctx_1024, L0_xattn_key_down, L0_xattn_query_down, L0_xattn_query_down_bias, L0_xattn_value_down, L0_xattn_value_up, L0_attn_Wq, L0_attn_Wk, L0_attn_Wv, L0_attn_Wo, L0_attn_lambda_q1, L0_attn_lambda_k1, L0_attn_lambda_q2, L0_attn_lambda_k2, L0_attn_gamma, L0_attn_beta, L0_ffn_Wq, L0_ffn_Wk, L0_ffn_Wv, L0_ffn_Wo, L0_ffn_g1, L0_ffn_b1, L0_ffn_g2, L0_ffn_b2, L0_ffn_Wg, L0_ffn_W1, L0_ffn_W2, L1_xattn_Wq, L1_xattn_bq, L1_xattn_Wk, L1_xattn_bk, L1_xattn_Wv, L1_xattn_bv, L1_xattn_Wo, L1_xattn_bo, L1_attn_Wq, L1_attn_Wk, L1_attn_Wv, L1_attn_Wo, L1_attn_bo, L1_attn_proj, L1_ffn_Win, L1_ffn_bin_, L1_ffn_W1, L1_ffn_b1, L1_ffn_W2, L1_ffn_b2, L1_ffn_Wout, L1_ffn_bout):
    import jax
    import jax.numpy as jnp

    def _L0_xattn_ref(query_tokens, key_tokens, key_down, query_down, query_down_bias, value_down, value_up):
        import jax, jax.numpy as jnp
        import numpy as np
        NOT_EPSILON = 1.0
        W_SCALE = 0.05
        H, T, A, C = (8, 512, 64, 128)

        def swishmax(x, axis):
            m = jnp.max(x, axis=axis, keepdims=True)
            xe = x * jnp.exp(x - m)
            return xe / (jnp.sum(jnp.abs(xe), axis=axis, keepdims=True) + NOT_EPSILON)
        k = jnp.einsum('bkt,hta->bhka', key_tokens, key_down)
        q = jnp.einsum('bqt,hta->bhqa', query_tokens, query_down) + query_down_bias[None]
        logits = jnp.einsum('bhka,bhqa->bhkq', k, q)
        attn = swishmax(logits, axis=-2)
        vs = jnp.einsum('bhkq,bkt->bhqt', attn, key_tokens)
        vs = jnp.einsum('bhqc,hct->bhqt', jnp.einsum('bhqt,htc->bhqc', vs, value_down), value_up)
        return vs.sum(axis=1)

    def _L0_attn_ref(x, Wq, Wk, Wv, Wo, lambda_q1, lambda_k1, lambda_q2, lambda_k2, gamma, beta):
        import jax, jax.numpy as jnp
        import numpy as np
        import math
        DIM = 512
        NUM_HEADS = 16
        HEAD_DIM = DIM // NUM_HEADS
        LAYER_IDX = 12
        LAMBDA_INIT = 0.8 - 0.6 * math.exp(-0.3 * (LAYER_IDX - 1))
        LN_EPS = 1e-05
        B, S, _ = x.shape
        scaling = HEAD_DIM ** (-0.5)
        Q = (x @ Wq).reshape(B, S, NUM_HEADS, 2 * HEAD_DIM).transpose(0, 2, 1, 3)
        K = (x @ Wk).reshape(B, S, NUM_HEADS, 2 * HEAD_DIM).transpose(0, 2, 1, 3)
        V = (x @ Wv).reshape(B, S, NUM_HEADS, HEAD_DIM).transpose(0, 2, 1, 3)
        lamb = jnp.exp(jnp.sum(lambda_q1 * lambda_k1)) - jnp.exp(jnp.sum(lambda_q2 * lambda_k2)) + LAMBDA_INIT
        Q1, Q2 = jnp.split(Q, 2, axis=-1)
        K1, K2 = jnp.split(K, 2, axis=-1)
        A1 = jnp.einsum('bhqd,bhkd->bhqk', Q1, K1) * scaling
        A2 = jnp.einsum('bhqd,bhkd->bhqk', Q2, K2) * scaling
        attn = jax.nn.softmax(A1, axis=-1) - lamb * jax.nn.softmax(A2, axis=-1)
        out = jnp.einsum('bhqk,bhkd->bhqd', attn, V)
        out = out.transpose(0, 2, 1, 3).reshape(B, S, DIM)
        out = out @ Wo
        mu = jnp.mean(out, axis=-1, keepdims=True)
        var = jnp.var(out, axis=-1, keepdims=True)
        out = (out - mu) * jax.lax.rsqrt(var + LN_EPS) * gamma + beta
        return out

    def _L0_ffn_ref(x, Wq, Wk, Wv, Wo, g1, b1, g2, b2, Wg, W1, W2):
        import jax, jax.numpy as jnp
        import numpy as np
        D_MODEL = 512
        N_HEADS = 16
        N_EXPERTS = 8
        TOP_K = 2
        EXPERT_HIDDEN = D_MODEL * 4 // N_EXPERTS

        def layer_norm(x, g, b, eps=1e-05):
            mu = jnp.mean(x, axis=-1, keepdims=True)
            var = jnp.var(x, axis=-1, keepdims=True)
            return (x - mu) * jax.lax.rsqrt(var + eps) * g + b
        B, S, D = x.shape
        H, dk = (N_HEADS, D // N_HEADS)
        xn = layer_norm(x, g1, b1)
        q = (xn @ Wq).reshape(B, S, H, dk).transpose(0, 2, 1, 3)
        k = (xn @ Wk).reshape(B, S, H, dk).transpose(0, 2, 1, 3)
        v = (xn @ Wv).reshape(B, S, H, dk).transpose(0, 2, 1, 3)
        scores = jnp.einsum('bhqd,bhkd->bhqk', q, k) / np.sqrt(dk)
        attn = jax.nn.softmax(scores, axis=-1)
        o = jnp.einsum('bhqk,bhkd->bhqd', attn, v)
        o = o.transpose(0, 2, 1, 3).reshape(B, S, D) @ Wo
        x = x + o
        xn2 = layer_norm(x, g2, b2)
        xf = xn2.reshape(B * S, D)
        gate = xf @ Wg
        topv, topi = jax.lax.top_k(gate, TOP_K)
        probs = jax.nn.softmax(topv, axis=-1)
        cw = jnp.sum(jax.nn.one_hot(topi, N_EXPERTS, dtype=xf.dtype) * probs[..., None], axis=1)
        h = jax.nn.relu(jnp.einsum('td,edh->teh', xf, W1))
        y = jnp.einsum('teh,ehd->ted', h, W2)
        moe = jnp.einsum('ted,te->td', y, cw).reshape(B, S, D)
        return x + moe

    def _L1_xattn_ref(query, key, value, Wq, bq, Wk, bk, Wv, bv, Wo, bo):
        import jax, jax.numpy as jnp
        import numpy as np
        D_MODEL = 512
        NUM_HEADS = 16
        HEAD_DIM = D_MODEL // NUM_HEADS
        B, T, _ = query.shape
        S = key.shape[1]
        q = query @ Wq.T + bq
        k = key @ Wk.T + bk
        v = value @ Wv.T + bv
        q = q.reshape(B, T, NUM_HEADS, HEAD_DIM).transpose(0, 2, 1, 3)
        k = k.reshape(B, S, NUM_HEADS, HEAD_DIM).transpose(0, 2, 1, 3)
        v = v.reshape(B, S, NUM_HEADS, HEAD_DIM).transpose(0, 2, 1, 3)
        scale = 1.0 / jnp.sqrt(jnp.asarray(HEAD_DIM, q.dtype))
        scores = jnp.einsum('bhtd,bhsd->bhts', q, k) * scale
        attn = jax.nn.softmax(scores, axis=-1)
        ctx = jnp.einsum('bhts,bhsd->bhtd', attn, v)
        ctx = ctx.transpose(0, 2, 1, 3).reshape(B, T, D_MODEL)
        return ctx @ Wo.T + bo

    def _L1_attn_ref(x, Wq, Wk, Wv, Wo, bo, proj):
        import jax, jax.numpy as jnp
        import numpy as np
        import math
        EPS = 1e-06

        def favorplus_features(x, proj):
            xw = jnp.einsum('bhtd,hmd->bhtm', x, proj)
            xw = xw - jnp.max(xw, axis=-1, keepdims=True)
            x_norm_sq = jnp.sum(x * x, axis=-1, keepdims=True)
            return jnp.exp(xw) * jnp.exp(-0.5 * x_norm_sq) + EPS
        B, T, d = x.shape
        h, m, dk = proj.shape

        def heads(W):
            y = jnp.einsum('btd,ed->bte', x, W)
            return y.reshape(B, T, h, dk).transpose(0, 2, 1, 3)
        Q = heads(Wq) / math.sqrt(dk)
        K = heads(Wk) / math.sqrt(dk)
        V = heads(Wv)
        inv_sqrt_m = 1.0 / math.sqrt(m)
        phiQ = favorplus_features(Q, proj) * inv_sqrt_m
        phiK = favorplus_features(K, proj) * inv_sqrt_m
        KV = jnp.einsum('bhtm,bhtd->bhmd', phiK, V)
        Ksum = jnp.sum(phiK, axis=2)
        num = jnp.einsum('bhtm,bhmd->bhtd', phiQ, KV)
        den = jnp.einsum('bhtm,bhm->bht', phiQ, Ksum)[..., None] + EPS
        out_heads = num / den
        merged = out_heads.transpose(0, 2, 1, 3).reshape(B, T, d)
        return jnp.einsum('btd,ed->bte', merged, Wo) + bo

    def _L1_ffn_ref(x, Win, bin_, W1, b1, W2, b2, Wout, bout):
        import jax, jax.numpy as jnp
        import numpy as np
        D_MODEL = 512
        M = 64
        INNER = 16
        s = jnp.einsum('btd,dm->btm', x, Win) + bin_
        h = jax.nn.relu(s[..., None] * W1 + b1)
        g = jnp.einsum('btmh,mh->btm', h, W2) + b2
        out = jnp.einsum('btm,md->btd', g, Wout) + bout
        return out
    x = x + _L0_xattn_ref(_layernorm(x, axis=-1), ctx_1024, L0_xattn_key_down, L0_xattn_query_down, L0_xattn_query_down_bias, L0_xattn_value_down, L0_xattn_value_up)
    x = x + _L0_attn_ref(_layernorm(x, axis=-1), L0_attn_Wq, L0_attn_Wk, L0_attn_Wv, L0_attn_Wo, L0_attn_lambda_q1, L0_attn_lambda_k1, L0_attn_lambda_q2, L0_attn_lambda_k2, L0_attn_gamma, L0_attn_beta)
    x = x + _L0_ffn_ref(_layernorm(x, axis=-1), L0_ffn_Wq, L0_ffn_Wk, L0_ffn_Wv, L0_ffn_Wo, L0_ffn_g1, L0_ffn_b1, L0_ffn_g2, L0_ffn_b2, L0_ffn_Wg, L0_ffn_W1, L0_ffn_W2)
    x = x + _L1_xattn_ref(_layernorm(x, axis=-1), ctx_1024, ctx_1024, L1_xattn_Wq, L1_xattn_bq, L1_xattn_Wk, L1_xattn_bk, L1_xattn_Wv, L1_xattn_bv, L1_xattn_Wo, L1_xattn_bo)
    x = x + _L1_attn_ref(_layernorm(x, axis=-1), L1_attn_Wq, L1_attn_Wk, L1_attn_Wv, L1_attn_Wo, L1_attn_bo, L1_attn_proj)
    x = x + _L1_ffn_ref(_layernorm(x, axis=-1), L1_ffn_Win, L1_ffn_bin_, L1_ffn_W1, L1_ffn_b1, L1_ffn_W2, L1_ffn_b2, L1_ffn_Wout, L1_ffn_bout)
    return x

_drawn_inputs = setup_inputs


def setup_inputs(seed=0):
    import zlib

    import numpy as np

    out = dict(_drawn_inputs(seed))
    spreads = {'L0_attn_gamma': (1.0, 0.2),
     'L0_attn_beta': (0.0, 0.1),
     'L0_ffn_g1': (1.0, 0.2),
     'L0_ffn_b1': (0.0, 0.1),
     'L0_ffn_g2': (1.0, 0.2),
     'L0_ffn_b2': (0.0, 0.1),
     'L1_xattn_bq': (0.0, 0.8),
     'L1_xattn_bk': (0.0, 2.0),
     'L1_xattn_bv': (0.0, 0.309),
     'L1_xattn_bo': (0.0, 0.307),
     'L1_attn_bo': (0.0, 0.325)}
    factors = {'L0_attn_lambda_q2': 3.853,
     'L0_attn_lambda_k2': 7.288,
     'L1_attn_Wq': 64.0,
     'L1_attn_Wk': 39.216,
     'L1_attn_proj': 59.648,
     'L1_ffn_Win': 3.181,
     'L1_ffn_bin_': 8.0,
     'L1_ffn_W1': 3.184,
     'L1_ffn_bout': 3.09,
     'L0_attn_lambda_k1': 3.734,
     'L1_attn_Wv': 64.0,
     'L1_attn_Wo': 64.0}
    for name, (base, spread) in spreads.items():
        noise = np.random.default_rng([zlib.crc32(name.encode()), seed]).standard_normal(out[name].shape)
        drawn = base * np.exp(spread * noise) if base else spread * noise
        out[name] = jnp.asarray(drawn.astype(out[name].dtype))
    for name, factor in factors.items():
        out[name] = (out[name] * factor).astype(out[name].dtype)
    return out
```

```python
import math
from contextlib import ExitStack

import concourse.bass as bass
from concourse import mybir

F32 = mybir.dt.float32
I32 = mybir.dt.int32
U32 = mybir.dt.uint32
ALU = mybir.AluOpType
ACT = mybir.ActivationFunctionType
AX = mybir.AxisListType

P = 128
B = 8
D = 512
DC = D // P
NK = 2048
CH = 512
NCH = NK // CH
KT = NK // P
LN_EPS = 1e-5
RSQRT_SEED = 0x5F3759DF
RSQRT_STEPS = 3


class Ring:

    def __init__(self, banks, full, out, order):
        self.banks, self.full, self.out, self.n = banks, full, out, len(order)
        self.at = {key: k for k, key in enumerate(order)}
        assert len(self.at) == len(order) and self.n % len(banks) == 0

    def bank(self, key):
        return self.banks[self.at[key] % len(self.banks)]

    def count(self, turn, key):
        return turn * self.n + self.at[key] + 1

    def landed(self, turn, key):
        return self.count(turn, key) + len(self.banks)


class Chain:

    def __init__(self, engine, sem, per_turn=0, turn=0):
        self.engine, self.sem, self.per_turn, self.base, self.n = engine, sem, per_turn, turn * per_turn, 0

    def __call__(self, instruction):
        self.n += 1
        instruction.then_inc(self.sem, 1)
        self.engine.wait_ge(self.sem, self.base + self.n)

    def hold(self):
        self.engine.sem_inc(self.sem, 1)
        self.n += 1

    def close(self):
        assert self.n == self.per_turn, (self.sem, self.n, self.per_turn)


class Space:

    def __init__(self, nc, ctx, phase):
        self.nc, self.ctx, self.phase = nc, ctx, phase

    def sb(self, name, shape, dtype=F32):
        return self.ctx.enter_context(self.nc.sbuf_tensor(f"{self.phase}_{name}", shape, dtype))

    def ps(self, name, shape, dtype=F32):
        return self.ctx.enter_context(self.nc.psum_tensor(f"{self.phase}_{name}", shape, dtype))

    def sem(self, name):
        return self.ctx.enter_context(self.nc.semaphore(f"{self.phase}_{name}"))


def rsqrt(nc, link, var, tmp, y, eps):
    link(nc.vector.tensor_scalar(var, var, eps, None, ALU.add))
    link(nc.vector.tensor_scalar(tmp.bitcast(U32), var.bitcast(U32), 1, None, ALU.logical_shift_right))
    link(nc.vector.tensor_scalar(y.bitcast(I32), tmp.bitcast(I32), -1.0, float(RSQRT_SEED), ALU.mult, ALU.add))
    for _ in range(RSQRT_STEPS):
        link(nc.vector.tensor_tensor(tmp, y, y, ALU.mult))
        link(nc.vector.tensor_tensor(tmp, tmp, var, ALU.mult))
        link(nc.vector.tensor_scalar(tmp, tmp, -0.5, 1.5, ALU.mult, ALU.add))
        link(nc.vector.tensor_tensor(y, y, tmp, ALU.mult))


LN_LINKS = 1 + 2 + 3 + 4 * RSQRT_STEPS


def layer_norm(nc, link, out, x, stats, mv, tmp, y):
    link(nc.vector.bn_stats(stats, x))
    link.hold()
    link(nc.vector.bn_aggr(mv, stats))
    rsqrt(nc, link, mv[:, 1:2], tmp, y, LN_EPS)
    return nc.vector.tensor_scalar(out, x, mv[:, 0:1], y, ALU.subtract, ALU.mult)


def columns(tile, turn):
    return tile[:, bass.ds(turn, 1), :].rearrange("p a d -> p (a d)")


def load(engine, dst, src, sem):
    engine.dma_start(dst, src.rearrange("(c p) n -> p c n", p=P)).then_inc(sem, 16)


def halves(bank):
    return bank[:, 0:2 * P].rearrange("p (c q) -> p c q", q=P)


def broadcast(row):
    return row.partition_broadcast(P)


def merged(main, extra):
    out, used = [], 0
    for n, step in enumerate(main):
        out.append(step)
        upto = (n + 1) * len(extra) // len(main)
        out += extra[used:upto]
        used = upto
    return out


def tile_stats(nc, link, x, stats, mv, tmp, rstd, var):
    for b in range(B):
        last = nc.vector.bn_stats(stats[:, b, :], x[:, b, :])
    link(last)
    for b in range(B):
        last = nc.vector.bn_aggr(mv[:, b, :], stats[:, b, :])
    link(last)
    link(nc.vector.tensor_copy(var, mv[:, :, 1]))
    rsqrt(nc, link, var, tmp, rstd, LN_EPS)


STATS_LINKS = 3 + 3 + 4 * RSQRT_STEPS


def tile_at(tile, turn, n=1):
    return tile[:, bass.ds(turn * n, n)]


def wait_tiles(engine, turn, rings, fill, *reads):
    need = {}
    for key in (fill, *reads):
        ring = next(r for r in rings if key in r.at)
        count = ring.at[key] + 1 + (len(ring.banks) if key is not fill else 0)
        need[ring.out] = (ring.n, max(count, need.get(ring.out, (0, 0))[1]))
    for sem, (per_turn, count) in need.items():
        engine.wait_ge(sem, turn * per_turn + count)


def swishmax_context(nc, x_dram, x_sb, ident, ctx_dram, ctx_t_dram, a, vs_dram):
    H, A = 8, 64
    HG = 4
    NG = H // HG
    PER = P // A
    with ExitStack() as ctx:
        s = Space(nc, ctx, "swishmax")
        w_key = s.sb("w_key", [P, DC, H * A])
        w_query = s.sb("w_query", [P, DC, H * A])
        q_bias = s.sb("q_bias", [P, DC])
        context = s.sb("context", [P, KT, D])
        context_t = s.sb("context_t", [P, 2, DC, CH])
        keys_t = s.sb("keys_t", [P, DC, NK])
        weights_t = s.sb("weights_t", [P, KT, HG * P])
        queries_t = s.sb("queries_t", [P, H, P])
        weights = s.sb("weights", [P, 2, NK])
        unused = s.sb("unused", [P, NK])
        values_t = s.sb("values_t", [P, DC, HG * P])
        hidden = s.sb("hidden", [P, D])
        hidden_t = s.sb("hidden_t", [P, DC, P])
        stats, mv = s.sb("stats", [P, B, 6]), s.sb("mv", [P, B, 2])
        var, tmp, rstd, means = (s.sb(n, [P, B]) for n in ("var", "tmp", "rstd", "means"))
        part_max = s.sb("part_max", [P, 2, NCH])
        neg_max = s.sb("neg_max", [P, 2])
        total = s.sb("total", [P, 2])
        scale = s.sb("scale", [P, 2])
        bank_a = [s.ps(f"bank_a{n}", [P, CH]) for n in range(2)]
        bank_d = [s.ps(f"bank_d{n}", [P, CH]) for n in range(2)]
        score = s.ps("score", [P, NK])

        loaded = s.sem("loaded")
        zeroed = s.sem("zeroed")
        normed_x = s.sem("normed_x")
        ctx_landed = [s.sem(f"ctx_landed{c}") for c in range(NCH)]
        ctx_t_landed = [s.sem(f"ctx_t_landed{c}") for c in range(2)]
        ctx_used = s.sem("ctx_used")
        full_a, out_a = s.sem("full_a"), s.sem("out_a")
        full_d, out_d = s.sem("full_d"), s.sem("out_d")
        scored = s.sem("scored")
        maxed = s.sem("maxed")
        exped = s.sem("exped")
        weighted = s.sem("weighted")
        summed = s.sem("summed")
        scaled = s.sem("scaled")
        last_full = s.sem("last_full")
        last_out = s.sem("last_out")
        stored, values_free = s.sem("stored"), s.sem("values_free")
        chain, chain_ln = s.sem("chain"), s.sem("chain_ln")
        LINKS = 3 * H

        order = [("hidden", 0), ("hidden", 1), ("query", 0), ("query", 1)]
        order += [("key", c, m) for c in range(NCH) for m in range(DC)]
        for h in range(1, H + 1):
            order += [("turned", h - 1, n) for n in range(NCH)]
            if h % HG == 0 and h < H:
                order += [("value", t) for t in range(DC)]
        ring_a = Ring(bank_a, full_a, out_a, order[0::2])
        ring_d = Ring(bank_d, full_d, out_d, order[1::2])

        def ring(key):
            return ring_a if key in ring_a.at else ring_d

        with nc.Block() as block:

            @block.sync
            def _(sp):
                load(sp, w_key[:], a["key_down"], loaded)
                load(sp, w_query[:], a["query_down"], loaded)
                sp.dma_start(q_bias[:], a["query_bias"]).then_inc(loaded, 16)
                for b in range(B):
                    sp.dma_start(x_sb[:, b, :], x_dram[b]).then_inc(loaded, 16)
                def load_context(b, c):
                    sp.dma_start(context[:, 4 * c:4 * c + 4, :], ctx_dram[bass.ds(b * NCH + c, 1)]
                                 .rearrange("a (k p) d -> p (a k) d", p=P)).then_inc(ctx_landed[c], 16)

                def load_context_t(b, c):
                    sp.dma_start(context_t[:, c % 2], ctx_t_dram[bass.ds(b * NCH + c, 1)]
                                 .rearrange("a (t p) k -> p (a t) k", p=P)).then_inc(ctx_t_landed[c % 2], 16)

                def projected(b, c):
                    sp.wait_ge(full_d, ring_d.count(b, ("key", c, DC - 1)))

                load_context_t(0, 0)
                load_context_t(0, 1)
                for c in range(NCH):
                    load_context(0, c)
                with sp.Fori(0, B - 1) as b:
                    for c in range(NCH):
                        projected(b, c)
                        load_context_t(b + (c + 2) // NCH, (c + 2) % NCH)
                    for c in range(NCH):
                        if c < NCH - 1:
                            sp.wait_ge(ctx_used, b * (NCH - 1) + c + 1)
                        else:
                            sp.wait_ge(last_full, b * DC + DC)
                        load_context(b + 1, c)
                for c in range(NCH - 2):
                    projected(B - 1, c)
                    load_context_t(B - 1, c + 2)

            @block.gpsimd
            def _(pool):
                pool.sem_inc(values_free, 1)
                with pool.Fori(0, B) as b:
                    for g in range(NG):
                        if g < NG - 1:
                            pool.wait_ge(out_a, ring_a.landed(b, ("value", 2)))
                            pool.wait_ge(out_d, ring_d.landed(b, ("value", 3)))
                        else:
                            pool.wait_ge(last_out, b * DC + DC + 1)
                        pool.dma_start(vs_dram[bass.ds(b * NG + g, 1)].rearrange("a (t p) q -> p (a t) q", p=P),
                                       values_t[:]).then_inc(stored, 16)
                        pool.wait_ge(stored, b * 16 * NG + 16 * g + 16)
                        pool.sem_inc(values_free, 1)

            @block.scalar
            def _(act):
                act.sem_inc(out_a, 2)
                act.sem_inc(last_out, 1)
                act.wait_ge(loaded, 16 * (3 + B))
                act.wait_ge(zeroed, 1)
                with act.Fori(0, B) as b:
                    act.wait_ge(full_a, ring_a.count(b, ("hidden", 0)))
                    nc.scalar.copy(hidden_t[:, 0:2, :], halves(ring_a.bank(("hidden", 0)))).then_inc(out_a, 1)
                    act.wait_ge(full_a, ring_a.count(b, ("query", 0)))
                    for h in range(H // 2):
                        r, m = A * (h % PER), h // PER
                        last = nc.scalar.activation(queries_t[r:r + A, h, :], ring_a.bank(("query", 0))[r:r + A, m * P:(m + 1) * P],
                                                    ACT.Identity, bias=q_bias[r:r + A, m:m + 1])
                    last.then_inc(out_a, 1)
                    for c in range(NCH):
                        for m in range(0, DC, 2):
                            key = ("key", c, m)
                            act.wait_ge(full_a, ring_a.count(b, key))
                            nc.scalar.copy(keys_t[:, m, c * CH:(c + 1) * CH], ring_a.bank(key)[:]).then_inc(out_a, 1)

                    def evict_turned(h):
                        for n in range(0, NCH, 2):
                            key = ("turned", h, n)
                            act.wait_ge(full_a, ring_a.count(b, key))
                            nc.scalar.copy(weights_t[:, 4 * n:4 * n + 4, (h % HG) * P:(h % HG + 1) * P],
                                           ring_a.bank(key)[:].rearrange("p (k q) -> p k q", q=P)).then_inc(out_a, 1)

                    for h in range(H):
                        if h == HG:
                            evict_turned(h - 1)
                        act.wait_ge(maxed, b * H + h + 1)
                        for c in range(NCH):
                            cols = slice(c * CH, (c + 1) * CH)
                            nc.scalar.activation(weights[:, h % 2, cols], score[:, cols], ACT.Exp,
                                                 bias=neg_max[:, h % 2:h % 2 + 1]).then_inc(exped, 1)
                        if h % HG:
                            evict_turned(h - 1)
                        if h == HG:
                            act.wait_ge(values_free, b * NG + 1)
                            for t in range(0, DC, 2):
                                key = ("value", t)
                                act.wait_ge(full_a, ring_a.count(b, key))
                                nc.scalar.copy(values_t[:, t, :], ring_a.bank(key)[:]).then_inc(out_a, 1)
                        act.wait_ge(weighted, (b * H + h) * NCH + 2 * NCH)
                        nc.scalar.activation(unused[:], weights[:, h % 2, :], ACT.Abs,
                                             accum_out=total[:, h % 2:h % 2 + 1]).then_inc(summed, 1)
                    evict_turned(H - 1)
                    act.wait_ge(values_free, b * NG + NG)
                    for t in range(DC):
                        act.wait_ge(last_full, b * DC + t + 1)
                        nc.scalar.copy(values_t[:, t, :], score[:, t * CH:(t + 1) * CH]).then_inc(last_out, 1)

            @block.vector
            def _(dve):
                dve.sem_inc(out_d, 2)
                dve.sem_inc(weighted, NCH)
                nc.vector.memset(queries_t[:], 0.0).then_inc(zeroed, 1)
                dve.wait_ge(loaded, 16 * (3 + B))
                first = Chain(dve, chain_ln)
                tile_stats(nc, first, x_sb, stats, mv, tmp[:], rstd[:], var[:])
                first(nc.vector.tensor_copy(means[:], mv[:, :, 0]))
                dve.wait_ge(zeroed, 1)
                with dve.Fori(0, B) as b:
                    link = Chain(dve, chain, LINKS, b)
                    nc.vector.tensor_scalar(hidden[:], columns(x_sb, b), tile_at(means, b), tile_at(rstd, b),
                                            ALU.subtract, ALU.mult).then_inc(normed_x, 1)
                    dve.wait_ge(full_d, ring_d.count(b, ("hidden", 1)))
                    nc.vector.tensor_copy(hidden_t[:, 2:4, :], halves(ring_d.bank(("hidden", 1)))).then_inc(out_d, 1)
                    dve.wait_ge(full_d, ring_d.count(b, ("query", 1)))
                    for h in range(H // 2, H):
                        r, m = A * (h % PER), h // PER
                        last = nc.vector.tensor_scalar(queries_t[r:r + A, h, :], ring_d.bank(("query", 1))[r:r + A, (m - 2) * P:(m - 1) * P],
                                                       q_bias[r:r + A, m:m + 1], None, ALU.add)
                    last.then_inc(out_d, 1)
                    for c in range(NCH):
                        for m in range(1, DC, 2):
                            key = ("key", c, m)
                            dve.wait_ge(full_d, ring_d.count(b, key))
                            nc.vector.tensor_copy(keys_t[:, m, c * CH:(c + 1) * CH], ring_d.bank(key)[:]).then_inc(out_d, 1)

                    def evict_turned(h):
                        for n in range(1, NCH, 2):
                            key = ("turned", h, n)
                            dve.wait_ge(full_d, ring_d.count(b, key))
                            nc.vector.tensor_copy(weights_t[:, 4 * n:4 * n + 4, (h % HG) * P:(h % HG + 1) * P],
                                                  ring_d.bank(key)[:].rearrange("p (k q) -> p k q", q=P)).then_inc(out_d, 1)

                    for h in range(H):
                        e = h % 2
                        for c in range(NCH):
                            dve.wait_ge(scored, (b * H + h) * NCH + c + 1)
                            last = nc.vector.tensor_reduce(part_max[:, e, c:c + 1], score[:, c * CH:(c + 1) * CH], AX.X, ALU.max)
                        link(last)
                        nc.vector.tensor_reduce(neg_max[:, e:e + 1], part_max[:, e, :], AX.X, ALU.max, negate=True).then_inc(maxed, 1)
                        if h >= 1:
                            evict_turned(h - 1)
                        for c in range(NCH):
                            cols = slice(c * CH, (c + 1) * CH)
                            dve.wait_ge(exped, (b * H + h) * NCH + c + 1)
                            nc.vector.tensor_tensor(weights[:, e, cols], weights[:, e, cols], score[:, cols], ALU.mult).then_inc(weighted, 1)
                        if h == HG:
                            dve.wait_ge(values_free, b * NG + 1)
                            for t in range(1, DC, 2):
                                key = ("value", t)
                                dve.wait_ge(full_d, ring_d.count(b, key))
                                nc.vector.tensor_copy(values_t[:, t, :], ring_d.bank(key)[:]).then_inc(out_d, 1)
                        dve.wait_ge(summed, b * H + h + 1)
                        link(nc.vector.tensor_scalar(total[:, e:e + 1], total[:, e:e + 1], 1.0, None, ALU.add))
                        link(nc.vector.reciprocal(scale[:, e:e + 1], total[:, e:e + 1]))
                        for c in range(NCH):
                            cols = slice(c * CH, (c + 1) * CH)
                            nc.vector.tensor_scalar(weights[:, e, cols], weights[:, e, cols], scale[:, e:e + 1], None,
                                                    ALU.mult).then_inc(scaled, 1)
                    evict_turned(H - 1)
                    link.close()

            @block.tensor
            def _(pe):
                pe.wait_ge(loaded, 16 * (3 + B))
                with pe.Fori(0, B) as b:
                    def start(key):
                        r = ring(key)
                        pe.wait_ge(r.out, r.count(b, key))
                        return r.bank(key)

                    pe.wait_ge(normed_x, b + 1)
                    for n in range(2):
                        bank = start(("hidden", n))
                        for c in range(2):
                            last = nc.tensor.transpose(bank[:, c * P:(c + 1) * P],
                                                       hidden[:, (2 * n + c) * P:(2 * n + c + 1) * P], ident[:])
                        last.then_inc(ring(("hidden", n)).full, 1)
                    for n in range(2):
                        bank = start(("query", n))
                        pe.wait_ge(out_a, ring_a.landed(b, ("hidden", 0)))
                        pe.wait_ge(out_d, ring_d.landed(b, ("hidden", 1)))
                        for m in range(2):
                            for c in range(DC):
                                last = nc.tensor.matmul(bank[:, m * P:(m + 1) * P], w_query[:, c, (2 * n + m) * P:(2 * n + m + 1) * P],
                                                        hidden_t[:, c, :], start=c == 0, stop=c == DC - 1)
                        last.then_inc(ring(("query", n)).full, 1)
                    for c in range(NCH):
                        pe.wait_ge(ctx_t_landed[c % 2], b * 32 + 16 * (c // 2) + 16)
                        for m in range(DC):
                            key = ("key", c, m)
                            bank = start(key)
                            for t in range(DC):
                                last = nc.tensor.matmul(bank[:], w_key[:, t, m * P:(m + 1) * P], context_t[:, c % 2, t, :],
                                                        start=t == 0, stop=t == DC - 1)
                            last.then_inc(ring(key).full, 1)

                    def scores(h):
                        if h == 0:
                            pe.wait_ge(out_d, ring_d.landed(b, ("key", NCH - 1, DC - 1)))
                            pe.wait_ge(out_a, ring_a.landed(b, ("key", NCH - 1, DC - 2)))
                            pe.wait_ge(last_out, b * DC + 1)
                        for c in range(NCH):
                            pe.wait_ge(weighted, (b * H + h) * NCH + c + 1)
                            nc.tensor.matmul(score[:, c * CH:(c + 1) * CH], queries_t[:, h, :],
                                             keys_t[:, h // PER, c * CH:(c + 1) * CH], start=True, stop=True).then_inc(scored, 1)

                    def turned(h, k):
                        if k % 4 == 0:
                            key = ("turned", h, k // 4)
                            pe.wait_ge(ring(key).out, ring(key).landed(b, key))

                    def turn(h):
                        for n in range(NCH):
                            key = ("turned", h, n)
                            pe.wait_ge(scaled, (b * H + h) * NCH + n + 1)
                            bank = start(key)
                            for k in range(4):
                                last = nc.tensor.transpose(bank[:, k * P:(k + 1) * P],
                                                           weights[:, h % 2, (4 * n + k) * P:(4 * n + k + 1) * P], ident[:])
                            last.then_inc(ring(key).full, 1)

                    for h in range(H):
                        scores(h)
                        if h >= 1:
                            turn(h - 1)
                        if h == HG:
                            for c in range(NCH):
                                pe.wait_ge(ctx_landed[c], b * 16 + 16)
                            for t in range(DC):
                                key = ("value", t)
                                bank = start(key)
                                for k in range(KT):
                                    if t == 0:
                                        turned(h - 1, k)
                                    last = nc.tensor.matmul(bank[:], context[:, k, t * P:(t + 1) * P], weights_t[:, k, :],
                                                            start=k == 0, stop=k == KT - 1)
                                last.then_inc(ring(key).full, 1)
                    turn(H - 1)
                    for k in range(KT):
                        turned(H - 1, k)
                        for t in range(DC):
                            last = nc.tensor.matmul(score[:, t * CH:(t + 1) * CH], context[:, k, t * P:(t + 1) * P],
                                                    weights_t[:, k, :], start=k == 0, stop=k == KT - 1)
                            if k == KT - 1:
                                last.then_inc(last_full, 1)
                        if k % 4 == 3 and k < KT - 1:
                            last.then_inc(ctx_used, 1)


def swishmax_output(nc, x_sb, a, vs_dram):
    H, C = 8, 128
    HG = 4
    NG = H // HG
    TURNS = 2
    NB = B // TURNS
    with ExitStack() as ctx:
        s = Space(nc, ctx, "swishmax_out")
        down = s.sb("down", [P, H, DC, C])
        up = s.sb("up", [P, H, D])
        values_t = s.sb("values_t", [P, NG, NB, DC, HG * P])
        inner_t = s.sb("inner_t", [P, H, NB * P])
        bank_a = [s.ps(f"bank_a{n}", [P, NB * P]) for n in range(2)]
        bank_d = [s.ps(f"bank_d{n}", [P, D]) for n in range(2)]
        loaded = s.sem("loaded")
        landed = [s.sem(f"landed{g}") for g in range(NG)]
        full_a, out_a = s.sem("full_a"), s.sem("out_a")
        full_d, out_d = s.sem("full_d"), s.sem("out_d")
        ring_a = Ring(bank_a, full_a, out_a, [("inner", h) for h in range(H)])
        ring_d = Ring(bank_d, full_d, out_d, [("out", n) for n in range(NB)])

        with nc.Block() as block:

            @block.sync
            def _(sp):
                for h in range(H):
                    sp.dma_start(down[:, h], a["value_down"][h].rearrange("(t p) c -> p t c", p=P)).then_inc(loaded, 16)
                sp.dma_start(up[:], a["value_up"].rearrange("h c d -> c h d")).then_inc(loaded, 16)

                def load_values(turn, g):
                    for n in range(NB):
                        sp.dma_start(values_t[:, g, n], vs_dram[bass.ds((turn * NB + n) * NG + g, 1)]
                                     .rearrange("a (t p) q -> p (a t) q", p=P)).then_inc(landed[g], 16)

                for g in range(NG):
                    load_values(0, g)
                for turn in range(1, TURNS):
                    for g in range(NG):
                        sp.wait_ge(full_a, ring_a.count(turn - 1, ("inner", HG * g + HG - 1)))
                        load_values(turn, g)

            @block.scalar
            def _(act):
                act.sem_inc(out_a, 2)
                with act.Fori(0, TURNS) as i:
                    for h in range(H):
                        act.wait_ge(full_a, ring_a.count(i, ("inner", h)))
                        nc.scalar.copy(inner_t[:, h, :], ring_a.bank(("inner", h))[:]).then_inc(out_a, 1)

            @block.vector
            def _(dve):
                dve.sem_inc(out_d, 2)
                with dve.Fori(0, TURNS) as i:
                    for n in range(NB):
                        dve.wait_ge(full_d, ring_d.count(i, ("out", n)))
                        xt = columns(x_sb, i * NB + n)
                        nc.vector.tensor_tensor(xt, xt, ring_d.bank(("out", n))[:], ALU.add).then_inc(out_d, 1)

            @block.tensor
            def _(pe):
                pe.wait_ge(loaded, 16 * (H + 1))
                with pe.Fori(0, TURNS) as i:
                    for h in range(H):
                        g, r = h // HG, h % HG
                        pe.wait_ge(landed[g], i * 16 * NB + 16 * NB)
                        pe.wait_ge(out_a, ring_a.count(i, ("inner", h)))
                        for t in range(DC):
                            last = nc.tensor.matmul(ring_a.bank(("inner", h))[:].rearrange("p (n q) -> p n q", q=P), down[:, h, t, :],
                                                    values_t[:, g, :, t, r * P:(r + 1) * P], start=t == 0, stop=t == DC - 1)
                        last.then_inc(full_a, 1)
                    pe.wait_ge(out_a, ring_a.landed(i, ("inner", H - 1)))
                    for n in range(NB):
                        pe.wait_ge(out_d, ring_d.count(i, ("out", n)))
                        for h in range(H):
                            last = nc.tensor.matmul(ring_d.bank(("out", n))[:], inner_t[:, h, n * P:(n + 1) * P], up[:, h, :],
                                                    start=h == 0, stop=h == H - 1)
                        last.then_inc(full_d, 1)


def token_attention(nc, phase, source, ident, a, twin, finish):
    H, HD = 16, 32
    PAIR = 2
    STREAMS = 2 if twin else 1
    DQ = STREAMS * D
    QT = DQ // P
    SR = P // HD
    HT = SR // STREAMS
    NG = H // SR
    SCALE = 1.0 / math.sqrt(HD)
    LAMBDA_INIT = 0.8 - 0.6 * math.exp(-0.3 * (12 - 1))
    SLOTS = 4
    with ExitStack() as ctx:
        s = Space(nc, ctx, phase)
        w = {"q": s.sb("wq", [P, DC, DQ]), "k": s.sb("wk", [P, DC, DQ]), "v": s.sb("wv", [P, DC, D]), "o": s.sb("wo", [P, DC, D])}
        gain, offset = s.sb("gain", [P, D]), s.sb("offset", [P, D])
        hidden = s.sb("hidden", [P, PAIR, D])
        hidden_t = s.sb("hidden_t", [P, PAIR, DC, P])
        queries_t = s.sb("queries_t", [P, PAIR, QT, P])
        keys_t = s.sb("keys_t", [P, PAIR, QT, SR, P])
        values = s.sb("values", [P, PAIR, D])
        exps = s.sb("exps", [P, SLOTS, SR, P])
        weights = s.sb("weights", [P, PAIR, H, P])
        weights_t = s.sb("weights_t", [P, PAIR, H, P])
        heads_t = s.sb("heads_t", [P, PAIR, NG, P])
        result = s.sb("result", [P, D])
        stats = s.sb("stats", [P, B, 6])
        mv = s.sb("mv", [P, B, 2])
        means = s.sb("means", [P, B])
        own_stats, own_mv = s.sb("own_stats", [P, 6]), s.sb("own_mv", [P, 2])
        var, tmp, rstd = s.sb("var", [P, B]), s.sb("tmp", [P, B]), s.sb("rstd", [P, B])
        neg_max = s.sb("neg_max", [P, SLOTS, SR])
        total = s.sb("total", [P, SLOTS, SR])
        scale = s.sb("scale", [P, SLOTS, SR])
        lam_in = s.sb("lam_in", [P, 4, HD])
        lam = s.sb("lam", [P, 2])
        lam_exp = s.sb("lam_exp", [P, 2])
        minus_lam = s.sb("minus_lam", [P, 1])
        bank_a = [s.ps(f"bank_a{n}", [P, CH]) for n in range(2)]
        bank_d = [s.ps(f"bank_d{n}", [P, CH]) for n in range(2)]
        score = [s.ps(f"score{n}", [P, CH]) for n in range(SLOTS)]

        loaded = s.sem("loaded")
        w_loaded = {name: s.sem("loaded_" + name) for name in w}
        zeroed = s.sem("zeroed")
        lam_ready = s.sem("lam_ready")
        lam_exped = s.sem("lam_exped")
        normed_x = s.sem("normed_x")
        full_a, out_a = s.sem("full_a"), s.sem("out_a")
        full_d, out_d = s.sem("full_d"), s.sem("out_d")
        scored = s.sem("scored")
        maxed = s.sem("maxed")
        exped = s.sem("exped")
        scaled = s.sem("scaled")
        chain = s.sem("chain")
        chain_ln = s.sem("chain_ln")

        def project(j):
            return [(what, j, n) for what in ("query", "key") for n in range(STREAMS)] + [("value", j, 0)]

        def score_steps(j):
            out = []
            for m in range(QT):
                out += [("score", j, m)] + ([("scale", j, m - 1)] if m else [])
            return out + [("scale", j, QT - 1)]

        def output_steps(j):
            return [(what, j, g) for g in range(NG) for what in ("turned", "heads")] + [("output", j, 0)]

        steps = [("hidden", j, n) for j in range(PAIR) for n in range(2)] + project(0)
        steps += merged(score_steps(0), project(1)) + merged(score_steps(1), output_steps(0)) + output_steps(1)
        BY_SCALAR = {("hidden", 0), ("query", 0), ("query", 1), ("value", 0), ("turned", 0), ("turned", 2), ("heads", 0), ("heads", 2)}
        tiles = [t for t in steps if t[0] not in ("score", "scale")]
        ring_a = Ring(bank_a, full_a, out_a, [t for t in tiles if (t[0], t[2]) in BY_SCALAR])
        ring_d = Ring(bank_d, full_d, out_d, [t for t in tiles if (t[0], t[2]) not in BY_SCALAR])
        SCORES = PAIR * QT

        def ring(key):
            return ring_a if key in ring_a.at else ring_d

        LINKS = SCORES * (1 + (3 if twin else 1)) + PAIR * ((LN_LINKS + 3) if finish == "norm" else 0)
        LINKS += PAIR * (2 if a.get("g") is not None else 0)
        LOADS = 2 + (4 if twin else 0)

        with nc.Block() as block:

            @block.sync
            def _(sp):
                g, o = ("g", "b") if finish == "add" else ("gamma", "beta")
                sp.dma_start(gain[:], broadcast(a[g])).then_inc(loaded, 16)
                sp.dma_start(offset[:], broadcast(a[o])).then_inc(loaded, 16)
                if twin:
                    for n, name in enumerate(("lambda_q1", "lambda_k1", "lambda_q2", "lambda_k2")):
                        sp.dma_start(lam_in[:, n, :], broadcast(a[name])).then_inc(loaded, 16)
                for name in w:
                    load(sp, w[name][:], a["w" + name], w_loaded[name])

            def evict_heads(engine_copy, t, bank):
                _, j, g = t
                for r in range(SR):
                    rows = slice(r * HD, (r + 1) * HD)
                    last = engine_copy(heads_t[rows, j, g, :], bank[rows, r * P:(r + 1) * P])
                return last

            @block.scalar
            def _(act):
                act.sem_inc(out_a, 2)
                act.sem_inc(exped, SLOTS)
                if twin:
                    act.wait_ge(lam_ready, 1)
                    nc.scalar.activation(lam_exp[:], lam[:], ACT.Exp).then_inc(lam_exped, 1)
                with act.Fori(0, B // PAIR) as i:
                    for t in steps:
                        what, j, n = t
                        if what == "score":
                            k = j * QT + n
                            e = k % SLOTS
                            act.wait_ge(maxed, i * SCORES + k + 1)
                            act.wait_ge(scaled, i * SCORES + k + 1)
                            for r in range(SR):
                                last = nc.scalar.activation(exps[:, e, r, :], score[e][:, r * P:(r + 1) * P], ACT.Exp,
                                                            bias=neg_max[:, e, r:r + 1], scale=SCALE,
                                                            accum_out=total[:, e, r:r + 1])
                            last.then_inc(exped, 1)
                        elif t in ring_a.at:
                            act.wait_ge(full_a, ring_a.count(i, t))
                            bank = ring_a.bank(t)
                            if what == "hidden":
                                last = nc.scalar.copy(hidden_t[:, j, 0:2, :], halves(bank))
                            elif what == "query":
                                last = nc.scalar.copy(queries_t[:, j, 4 * n:4 * n + 4, :], bank[:].rearrange("p (m q) -> p m q", q=P))
                            elif what == "value":
                                last = nc.scalar.copy(values[:, j, :], bank[:])
                            elif what == "turned":
                                last = nc.scalar.copy(weights_t[:, j, 4 * n:4 * n + 4, :], bank[:].rearrange("p (h q) -> p h q", q=P))
                            elif what == "heads":
                                last = evict_heads(nc.scalar.copy, t, bank)
                            last.then_inc(out_a, 1)

            @block.vector
            def _(dve):
                dve.sem_inc(out_d, 2)
                dve.sem_inc(scaled, SLOTS)
                nc.vector.memset(keys_t[:], 0.0).then_inc(zeroed, 1)
                first = Chain(dve, chain_ln)
                tile_stats(nc, first, source, stats, mv, tmp[:], rstd[:], var[:])
                first(nc.vector.tensor_copy(means[:], mv[:, :, 0]))
                dve.wait_ge(loaded, 16 * LOADS)
                if twin:
                    for n in range(2):
                        first(nc.vector.tensor_tensor(lam_in[:, 2 * n, :], lam_in[:, 2 * n, :], lam_in[:, 2 * n + 1, :], ALU.mult))
                    for n in range(2):
                        last = nc.vector.tensor_reduce(lam[:, n:n + 1], lam_in[:, 2 * n, :], AX.X, ALU.add)
                    last.then_inc(lam_ready, 1)
                    dve.wait_ge(lam_exped, 1)
                    first(nc.vector.tensor_tensor(minus_lam[:], lam_exp[:, 1:2], lam_exp[:, 0:1], ALU.subtract))
                    first(nc.vector.tensor_scalar(minus_lam[:], minus_lam[:], LAMBDA_INIT, None, ALU.subtract))
                dve.wait_ge(zeroed, 1)
                with dve.Fori(0, B // PAIR) as i:
                    link = Chain(dve, chain, LINKS, i)

                    def output(t):
                        j = t[1]
                        bank = ring_d.bank(t)
                        if finish == "add":
                            xt = columns(source, i * PAIR + j)
                            return nc.vector.tensor_tensor(xt, xt, bank[:], ALU.add)
                        link(layer_norm(nc, link, result[:], bank[:], own_stats[:], own_mv[:], tmp[:, 0:1], var[:, 0:1]))
                        link(nc.vector.tensor_tensor(result[:], result[:], gain[:], ALU.mult))
                        link(nc.vector.tensor_tensor(result[:], result[:], offset[:], ALU.add))
                        xt = columns(source, i * PAIR + j)
                        return nc.vector.tensor_tensor(xt, xt, result[:], ALU.add)

                    for j in range(PAIR):
                        b = i * PAIR + j
                        norm = nc.vector.tensor_scalar(hidden[:, j, :], columns(source, b), tile_at(means, b),
                                                       tile_at(rstd, b), ALU.subtract, ALU.mult)
                        if a.get("g") is not None:
                            link(norm)
                            link(nc.vector.tensor_tensor(hidden[:, j, :], hidden[:, j, :], gain[:], ALU.mult))
                            norm = nc.vector.tensor_tensor(hidden[:, j, :], hidden[:, j, :], offset[:], ALU.add)
                        norm.then_inc(normed_x, 1)
                    for t in steps:
                        what, j, n = t
                        if what == "score":
                            k = j * QT + n
                            e = k % SLOTS
                            dve.wait_ge(scored, i * SCORES + k + 1)
                            link(nc.vector.tensor_reduce(neg_max[:, e, :], score[e][:].rearrange("p (r k) -> p r k", k=P),
                                                         AX.X, ALU.max, negate=True))
                            nc.vector.tensor_scalar(neg_max[:, e, :], neg_max[:, e, :], SCALE, None, ALU.mult).then_inc(maxed, 1)
                        elif what == "scale":
                            k = j * QT + n
                            e = k % SLOTS
                            dve.wait_ge(exped, i * SCORES + k + 1 + SLOTS)
                            link(nc.vector.reciprocal(scale[:, e, :], total[:, e, :]))
                            if twin:
                                for h in range(HT):
                                    last = nc.vector.tensor_scalar(scale[:, e, 2 * h + 1:2 * h + 2], scale[:, e, 2 * h + 1:2 * h + 2],
                                                                   minus_lam[:], None, ALU.mult)
                                link(last)
                                for h in range(HT):
                                    last = nc.vector.tensor_scalar(exps[:, e, 2 * h, :], exps[:, e, 2 * h, :],
                                                                   scale[:, e, 2 * h:2 * h + 1], None, ALU.mult)
                                link(last)
                                for h in range(HT):
                                    last = nc.vector.scalar_tensor_tensor(out=weights[:, j, HT * n + h, :], in0=exps[:, e, 2 * h + 1, :],
                                                                          scalar=scale[:, e, 2 * h + 1:2 * h + 2], in1=exps[:, e, 2 * h, :],
                                                                          op0=ALU.mult, op1=ALU.add)
                            else:
                                for h in range(HT):
                                    last = nc.vector.tensor_scalar(weights[:, j, HT * n + h, :], exps[:, e, h, :],
                                                                   scale[:, e, h:h + 1], None, ALU.mult)
                            last.then_inc(scaled, 1)
                        elif t in ring_d.at:
                            dve.wait_ge(full_d, ring_d.count(i, t))
                            bank = ring_d.bank(t)
                            if what == "hidden":
                                last = nc.vector.tensor_copy(hidden_t[:, j, 2:4, :], halves(bank))
                            elif what == "key":
                                for r in range(SR):
                                    rows = slice(r * HD, (r + 1) * HD)
                                    last = nc.vector.tensor_copy(keys_t[rows, j, 4 * n:4 * n + 4, r, :],
                                                                 bank[rows, :].rearrange("p (m q) -> p m q", q=P))
                            elif what == "turned":
                                last = nc.vector.tensor_copy(weights_t[:, j, 4 * n:4 * n + 4, :], bank[:].rearrange("p (h q) -> p h q", q=P))
                            elif what == "heads":
                                last = evict_heads(nc.vector.tensor_copy, t, bank)
                            elif what == "output":
                                last = output(t)
                            last.then_inc(out_d, 1)
                    link.close()

            @block.tensor
            def _(pe):
                with pe.Fori(0, B // PAIR) as i:
                    def landed(key):
                        r = ring(key)
                        pe.wait_ge(r.out, r.landed(i, key))

                    for t in steps:
                        what, j, n = t
                        if what == "scale":
                            continue
                        if what == "score":
                            k = j * QT + n
                            if n % 4 == 0:
                                landed(("query", j, n // 4))
                                landed(("key", j, n // 4))
                            pe.wait_ge(exped, i * SCORES + k + 1)
                            nc.tensor.matmul(score[k % SLOTS][:], queries_t[:, j, n, :], keys_t[:, j, n, :, :].rearrange("p r k -> p (r k)"),
                                             start=True, stop=True).then_inc(scored, 1)
                            continue
                        r = ring(t)
                        bank = r.bank(t)
                        reads = {"query": [("hidden", j, 0), ("hidden", j, 1)], "turned": [], "hidden": [],
                                 "heads": [("value", j, 0), ("turned", j, n)],
                                 "output": [("heads", j, NG - 2), ("heads", j, NG - 1)]}
                        reads["key"] = reads["value"] = reads["query"]
                        wait_tiles(pe, i, (ring_a, ring_d), t, *reads[what])
                        if what == "hidden":
                            pe.wait_ge(normed_x, i * PAIR + j + 1)
                            for c in range(2):
                                last = nc.tensor.transpose(bank[:, c * P:(c + 1) * P],
                                                           hidden[:, j, (2 * n + c) * P:(2 * n + c + 1) * P], ident[:])
                        elif what in ("query", "key"):
                            pe.wait_ge(w_loaded[what[0]], 16)
                            for m in range(4):
                                for c in range(DC):
                                    last = nc.tensor.matmul(bank[:, m * P:(m + 1) * P], w[what[0]][:, c, (4 * n + m) * P:(4 * n + m + 1) * P],
                                                            hidden_t[:, j, c, :], start=c == 0, stop=c == DC - 1)
                        elif what == "value":
                            pe.wait_ge(w_loaded["v"], 16)
                            for c in range(DC):
                                last = nc.tensor.matmul(bank[:], hidden_t[:, j, c, :], w["v"][:, c, :], start=c == 0, stop=c == DC - 1)
                        elif what == "turned":
                            pe.wait_ge(scaled, i * SCORES + j * QT + (4 * n + 3) // HT + 1 + SLOTS)
                            for h in range(4):
                                last = nc.tensor.transpose(bank[:, h * P:(h + 1) * P], weights[:, j, 4 * n + h, :], ident[:])
                        elif what == "heads":
                            last = nc.tensor.matmul(bank[:], values[:, j, n * P:(n + 1) * P],
                                                    weights_t[:, j, 4 * n:4 * n + 4, :].rearrange("p h q -> p (h q)"), start=True, stop=True)
                        elif what == "output":
                            pe.wait_ge(w_loaded["o"], 16)
                            for g in range(NG):
                                last = nc.tensor.matmul(bank[:], heads_t[:, j, g, :], w["o"][:, g, :], start=g == 0, stop=g == NG - 1)
                        last.then_inc(r.full, 1)


def norm_tiles(nc, x_sb, out):
    with ExitStack() as ctx:
        s = Space(nc, ctx, "norm")
        stats, mv = s.sb("stats", [P, B, 6]), s.sb("mv", [P, B, 2])
        var, tmp, rstd = s.sb("var", [P, B]), s.sb("tmp", [P, B]), s.sb("rstd", [P, B])
        chain = s.sem("chain")
        with nc.Block() as block:

            @block.vector
            def _(dve):
                link = Chain(dve, chain)
                tile_stats(nc, link, x_sb, stats, mv, tmp[:], rstd[:], var[:])
                for b in range(B):
                    nc.vector.tensor_scalar(out[:, b, :], x_sb[:, b, :], mv[:, b, 0:1], rstd[:, b:b + 1], ALU.subtract, ALU.mult)


def experts(nc, x_sb, mid, ident, a):
    E, F = 8, 256
    TURNS = 2
    NB = B // TURNS
    FT = E * F // P
    FE = F // P
    with ExitStack() as ctx:
        s = Space(nc, ctx, "experts")
        w1 = s.sb("w1", [P, E, DC, F])
        w2 = s.sb("w2", [P, E, FE, D])
        wg = s.sb("wg", [P, DC, E])
        gain, offset = s.sb("gain", [P, D]), s.sb("offset", [P, D])
        numbers = s.sb("numbers", [P, E])
        tokens = s.sb("tokens", [P, NB, D])
        tokens_t = s.sb("tokens_t", [P, DC, NB * P])
        inner_t = s.sb("inner_t", [P, FT, NB * P])
        stats, mv = s.sb("stats", [P, B, 6]), s.sb("mv", [P, B, 2])
        var, tmp, rstd, means = (s.sb(n, [P, B]) for n in ("var", "tmp", "rstd", "means"))
        gate = s.sb("gate", [P, NB, E])
        best = s.sb("best", [P, NB, E])
        best_at = s.sb("best_at", [P, NB, E], U32)
        best_no = s.sb("best_no", [P, NB, E])
        gap = s.sb("gap", [P, NB])
        gap_exp = s.sb("gap_exp", [P, NB])
        prob = s.sb("prob", [P, 2, NB])
        share = s.sb("share", [P, 2, NB, E])
        weight = s.sb("weight", [P, NB, E])
        bank_a = [s.ps(f"bank_a{n}", [P, CH]) for n in range(4)]
        bank_d = [s.ps(f"bank_d{n}", [P, CH]) for n in range(4)]
        loaded = s.sem("loaded")
        w1_loaded = [s.sem(f"loaded_w1_{e}") for e in range(E)]
        w2_loaded = [s.sem(f"loaded_w2_{e}") for e in range(E)]
        normed_x = s.sem("normed_x")
        gap_ready = s.sem("gap_ready")
        gap_exped = s.sem("gap_exped")
        full_a, out_a = s.sem("full_a"), s.sem("out_a")
        full_d, out_d = s.sem("full_d"), s.sem("out_d")
        chain, chain_ln = s.sem("chain"), s.sem("chain_ln")
        steps = [("token", n) for n in range(NB)] + [("gate", n) for n in range(NB)]
        steps += [("inner", f) for f in range(FT)] + [("expert", n, e) for e in range(E) for n in range(NB)]
        on_scalar = {t for t in steps if t[0] == "token" or (t[0] == "inner" and t[1] % 2 == 0)}
        ring_a = Ring(bank_a, full_a, out_a, [t for t in steps if t in on_scalar])
        ring_d = Ring(bank_d, full_d, out_d, [t for t in steps if t not in on_scalar])
        LINKS = 2 * NB + 10
        LOADS = 4

        with nc.Block() as block:

            @block.sync
            def _(sp):
                load(sp, wg[:], a["Wg"], loaded)
                sp.dma_start(gain[:], broadcast(a["g2"])).then_inc(loaded, 16)
                sp.dma_start(offset[:], broadcast(a["b2"])).then_inc(loaded, 16)
                sp.dma_start(numbers[:], broadcast(a["numbers"])).then_inc(loaded, 16)
                for e in range(E):
                    load(sp, w1[:, e], a["W1"][e], w1_loaded[e])
                for e in range(E):
                    load(sp, w2[:, e], a["W2"][e], w2_loaded[e])

            @block.scalar
            def _(act):
                act.sem_inc(out_a, 4)
                with act.Fori(0, TURNS) as i:
                    for t in ring_a.at:
                        act.wait_ge(full_a, ring_a.count(i, t))
                        if t[0] == "token":
                            nc.scalar.copy(tokens_t[:, :, t[1] * P:(t[1] + 1) * P],
                                           ring_a.bank(t)[:].rearrange("p (c q) -> p c q", q=P)).then_inc(out_a, 1)
                        else:
                            nc.scalar.activation(inner_t[:, t[1], :], ring_a.bank(t)[:], ACT.Relu).then_inc(out_a, 1)
                        if t == ("inner", 0):
                            act.wait_ge(gap_ready, i + 1)
                            nc.scalar.activation(gap_exp[:], gap[:], ACT.Exp).then_inc(gap_exped, 1)

            @block.vector
            def _(dve):
                dve.sem_inc(out_d, 4)
                first = Chain(dve, chain_ln)
                tile_stats(nc, first, mid, stats, mv, tmp[:], rstd[:], var[:])
                first(nc.vector.tensor_copy(means[:], mv[:, :, 0]))
                dve.wait_ge(loaded, 16 * LOADS)
                with dve.Fori(0, TURNS) as i:
                    link = Chain(dve, chain, LINKS, i)
                    for n in range(NB):
                        b = i * NB + n
                        link(nc.vector.tensor_scalar(tokens[:, n, :], columns(mid, b), tile_at(means, b), tile_at(rstd, b),
                                                     ALU.subtract, ALU.mult))
                        link(nc.vector.tensor_tensor(tokens[:, n, :], tokens[:, n, :], gain[:], ALU.mult))
                        nc.vector.tensor_tensor(tokens[:, n, :], tokens[:, n, :], offset[:], ALU.add).then_inc(normed_x, 1)
                    for n in range(NB):
                        t = ("gate", n)
                        dve.wait_ge(full_d, ring_d.count(i, t))
                        nc.vector.tensor_copy(gate[:, n, :], ring_d.bank(t)[:, 0:E]).then_inc(out_d, 1)
                    dve.wait_ge(out_d, ring_d.landed(i, ("gate", NB - 1)))
                    link.hold()
                    for n in range(NB):
                        last = nc.vector.max(best[:, n, :], gate[:, n, :])
                    link(last)
                    link.hold()
                    for n in range(NB):
                        last = nc.vector.max_index(best_at[:, n, :], best[:, n, :], gate[:, n, :])
                    link(last)
                    link(nc.vector.tensor_copy(best_no[:], best_at[:]))
                    nc.vector.tensor_tensor(gap[:], best[:, :, 1], best[:, :, 0], ALU.subtract).then_inc(gap_ready, 1)
                    dve.wait_ge(gap_exped, i + 1)
                    link(nc.vector.tensor_scalar(prob[:, 1, :], gap_exp[:], 1.0, None, ALU.add))
                    link(nc.vector.reciprocal(prob[:, 0, :], prob[:, 1, :]))
                    link(nc.vector.tensor_tensor(prob[:, 1, :], prob[:, 0, :], gap_exp[:], ALU.mult))
                    for n in range(NB):
                        for k in range(2):
                            last = nc.vector.tensor_scalar(share[:, k, n, :], numbers[:], best_no[:, n, k:k + 1], prob[:, k, n:n + 1],
                                                           ALU.is_equal, ALU.mult)
                    link(last)
                    link(nc.vector.tensor_tensor(weight[:], share[:, 0], share[:, 1], ALU.add))
                    for f in range(1, FT, 2):
                        t = ("inner", f)
                        dve.wait_ge(full_d, ring_d.count(i, t))
                        nc.vector.tensor_scalar(inner_t[:, f, :], ring_d.bank(t)[:], 0.0, None, ALU.max).then_inc(out_d, 1)
                    for e in range(E):
                        for n in range(NB):
                            t = ("expert", n, e)
                            dve.wait_ge(full_d, ring_d.count(i, t))
                            if e:
                                dve.wait_ge(out_d, ring_d.landed(i, ("expert", n, e - 1)))
                            acc = columns(mid, i * NB + n)
                            nc.vector.scalar_tensor_tensor(out=acc, in0=ring_d.bank(t)[:], scalar=weight[:, n, e:e + 1], in1=acc,
                                                           op0=ALU.mult, op1=ALU.add).then_inc(out_d, 1)
                    for n in range(NB):
                        dve.wait_ge(out_d, ring_d.landed(i, ("expert", n, E - 1)))
                        b = i * NB + n
                        nc.vector.tensor_tensor(columns(x_sb, b), columns(x_sb, b), columns(mid, b), ALU.add)
                    link.close()

            @block.tensor
            def _(pe):
                pe.wait_ge(loaded, 16 * LOADS)
                with pe.Fori(0, TURNS) as i:
                    for t in steps:
                        ring = ring_a if t in on_scalar else ring_d
                        bank = ring.bank(t)
                        if t[0] == "token":
                            wait_tiles(pe, i, (ring_a, ring_d), t)
                            pe.wait_ge(normed_x, i * NB + t[1] + 1)
                            for c in range(DC):
                                last = nc.tensor.transpose(bank[:, c * P:(c + 1) * P], tokens[:, t[1], c * P:(c + 1) * P], ident[:])
                        elif t[0] == "gate":
                            wait_tiles(pe, i, (ring_a, ring_d), t, ("token", t[1]))
                            for c in range(DC):
                                last = nc.tensor.matmul(bank[:, 0:E], tokens_t[:, c, t[1] * P:(t[1] + 1) * P], wg[:, c, :],
                                                        start=c == 0, stop=c == DC - 1)
                        elif t[0] == "inner":
                            wait_tiles(pe, i, (ring_a, ring_d), t, ("token", NB - 1))
                            e, f = t[1] // FE, t[1] % FE
                            pe.wait_ge(w1_loaded[e], 16)
                            for c in range(DC):
                                last = nc.tensor.matmul(bank[:], w1[:, e, c, f * P:(f + 1) * P], tokens_t[:, c, :],
                                                        start=c == 0, stop=c == DC - 1)
                        else:
                            _, n, e = t
                            wait_tiles(pe, i, (ring_a, ring_d), t, ("inner", e * FE), ("inner", e * FE + 1))
                            pe.wait_ge(w2_loaded[e], 16)
                            for f in range(FE):
                                last = nc.tensor.matmul(bank[:], inner_t[:, e * FE + f, n * P:(n + 1) * P], w2[:, e, f, :],
                                                        start=f == 0, stop=f == FE - 1)
                        last.then_inc(ring.full, 1)


def softmax_context(nc, x_sb, ident, ctx_t_dram, a):
    H, HD = 16, 32
    HG = P // HD
    NG = H // HG
    SCALE = 1.0 / math.sqrt(HD)
    with ExitStack() as ctx:
        s = Space(nc, ctx, "context")
        w = {name: s.sb("w" + name, [P, DC, D]) for name in ("q", "k", "v", "o")}
        bias = s.sb("bias", [P, 3, DC])
        bias_q = s.sb("bias_q", [P, DC])
        bias_o = s.sb("bias_o", [P, D])
        context_t = s.sb("context_t", [P, 2, DC, CH])
        keys_t = s.sb("keys_t", [P, DC, NK])
        values = s.sb("values", [P, KT, D])
        weights_t = s.sb("weights_t", [P, KT, HG * P])
        queries_t = s.sb("queries_t", [P, H, P])
        weights = s.sb("weights", [P, 2, NK])
        heads_t = s.sb("heads_t", [P, NG, P])
        hidden = s.sb("hidden", [P, D])
        hidden_t = s.sb("hidden_t", [P, DC, P])
        stats, mv = s.sb("stats", [P, B, 6]), s.sb("mv", [P, B, 2])
        var, tmp, rstd, means = (s.sb(n, [P, B]) for n in ("var", "tmp", "rstd", "means"))
        neg_max = s.sb("neg_max", [P, 2])
        part_max, part_total = s.sb("part_max", [P, 2, NCH]), s.sb("part_total", [P, 2, NCH])
        total = s.sb("total", [P, 2])
        scale = s.sb("scale", [P, 2])
        bank_a = [s.ps(f"bank_a{n}", [P, CH]) for n in range(3)]
        bank_d = [s.ps(f"bank_d{n}", [P, CH]) for n in range(1)]
        score = s.ps("score", [P, NK])

        loaded = s.sem("loaded")
        w_loaded = {name: s.sem("loaded_" + name) for name in w}
        zeroed = s.sem("zeroed")
        bias_scaled = s.sem("bias_scaled")
        normed_x = s.sem("normed_x")
        ctx_t_landed = [s.sem(f"ctx_t_landed{c}") for c in range(2)]
        full_a, out_a = s.sem("full_a"), s.sem("out_a")
        full_d, out_d = s.sem("full_d"), s.sem("out_d")
        scored = s.sem("scored")
        maxed = s.sem("maxed")
        exped = s.sem("exped")
        scaled = s.sem("scaled")
        shifted = s.sem("shifted")
        chain, chain_ln = s.sem("chain"), s.sem("chain_ln")
        LINKS = 3 * H + 1
        LOADS = 3 + 1

        BY_ACT = (0, 1, 2)
        LAST = 3
        order = [(what, c, m) for c in range(NCH) for what in ("key", "value") for m in range(DC)]
        order += [("turned", h, n) for h in range(H) for n in range(NCH)]
        by_scalar = [("hidden", 0), ("hidden", 1), ("query", 0)] + [key for key in order if key[-1] in BY_ACT]
        by_vector = [("query", 1)] + [key for key in order if key[-1] == LAST]
        for g in range(NG):
            by_vector.insert(by_vector.index(("turned", HG * g + HG - 1, NCH - 1)) + 1, ("heads", g))
        by_vector += [("output", 0), ("output", 1)]
        ring_a = Ring(bank_a, full_a, out_a, by_scalar)
        ring_d = Ring(bank_d, full_d, out_d, by_vector)

        def ring(key):
            return ring_a if key in ring_a.at else ring_d

        with nc.Block() as block:

            @block.sync
            def _(sp):
                for n, name in enumerate(("bq", "bk", "bv")):
                    sp.dma_start(bias[:, n, :], a[name]).then_inc(loaded, 16)
                sp.dma_start(bias_o[:], broadcast(a["bo"])).then_inc(loaded, 16)

                def load_context_t(b, c):
                    sp.dma_start(context_t[:, c % 2], ctx_t_dram[bass.ds(b * NCH + c, 1)]
                                 .rearrange("a (t p) k -> p (a t) k", p=P)).then_inc(ctx_t_landed[c % 2], 16)

                def projected(b, c):
                    sp.wait_ge(full_d, ring_d.count(b, ("value", c, DC - 1)))

                load(sp, w["q"][:], a["wq"], w_loaded["q"])
                load(sp, w["k"][:], a["wk"], w_loaded["k"])
                load_context_t(0, 0)
                load(sp, w["v"][:], a["wv"], w_loaded["v"])
                load_context_t(0, 1)
                load(sp, w["o"][:], a["wo"], w_loaded["o"])
                with sp.Fori(0, B - 1) as b:
                    for c in range(NCH):
                        projected(b, c)
                        load_context_t(b + (c + 2) // NCH, (c + 2) % NCH)
                for c in range(NCH - 2):
                    projected(B - 1, c)
                    load_context_t(B - 1, c + 2)

            @block.scalar
            def _(act):
                act.sem_inc(out_a, len(bank_a))
                act.sem_inc(exped, NCH)
                act.wait_ge(loaded, 16 * LOADS)
                act.wait_ge(zeroed, 1)
                act.wait_ge(bias_scaled, 1)
                with act.Fori(0, B) as b:
                    for n in range(2):
                        key = ("hidden", n)
                        act.wait_ge(full_a, ring_a.count(b, key))
                        nc.scalar.copy(hidden_t[:, 2 * n:2 * n + 2, :], halves(ring_a.bank(key))).then_inc(out_a, 1)
                    act.wait_ge(full_a, ring_a.count(b, ("query", 0)))
                    for h in range(H // 2):
                        r, m = HD * (h % HG), h // HG
                        last = nc.scalar.activation(queries_t[r:r + HD, h, :], ring_a.bank(("query", 0))[r:r + HD, m * P:(m + 1) * P],
                                                    ACT.Identity, bias=bias_q[r:r + HD, m:m + 1], scale=SCALE)
                    last.then_inc(out_a, 1)
                    for c in range(NCH):
                        for m in BY_ACT:
                            key = ("key", c, m)
                            act.wait_ge(full_a, ring_a.count(b, key))
                            nc.scalar.activation(keys_t[:, m, c * CH:(c + 1) * CH], ring_a.bank(key)[:],
                                                 ACT.Identity, bias=bias[:, 1, m:m + 1]).then_inc(out_a, 1)
                        for k in BY_ACT:
                            key = ("value", c, k)
                            act.wait_ge(full_a, ring_a.count(b, key))
                            nc.scalar.copy(values[:, 4 * c + k, :], ring_a.bank(key)[:]).then_inc(out_a, 1)

                    def evict_turned(h):
                        for n in BY_ACT:
                            key = ("turned", h, n)
                            act.wait_ge(full_a, ring_a.count(b, key))
                            nc.scalar.copy(weights_t[:, 4 * n:4 * n + 4, (h % HG) * P:(h % HG + 1) * P],
                                           ring_a.bank(key)[:].rearrange("p (k q) -> p k q", q=P)).then_inc(out_a, 1)

                    for h in range(H):
                        e = h % 2
                        if h % HG == 0 and h:
                            evict_turned(h - 1)
                        act.wait_ge(maxed, b * H + h + 1)
                        for c in range(NCH):
                            cols = slice(c * CH, (c + 1) * CH)
                            nc.scalar.activation(weights[:, e, cols], score[:, cols], ACT.Exp, bias=neg_max[:, e:e + 1],
                                                 accum_out=part_total[:, e, c:c + 1]).then_inc(exped, 1)
                        if h % HG:
                            evict_turned(h - 1)
                    evict_turned(H - 1)

            @block.vector
            def _(dve):
                dve.sem_inc(out_d, len(bank_d))
                nc.vector.memset(queries_t[:], 0.0).then_inc(zeroed, 1)
                first = Chain(dve, chain_ln)
                tile_stats(nc, first, x_sb, stats, mv, tmp[:], rstd[:], var[:])
                first(nc.vector.tensor_copy(means[:], mv[:, :, 0]))
                dve.wait_ge(loaded, 16 * LOADS)
                first(nc.vector.tensor_scalar(bias_q[:], bias[:, 0, :], SCALE, None, ALU.mult))
                dve.sem_inc(bias_scaled, 1)
                dve.wait_ge(zeroed, 1)
                with dve.Fori(0, B) as b:
                    link = Chain(dve, chain, LINKS, b)
                    nc.vector.tensor_scalar(hidden[:], columns(x_sb, b), tile_at(means, b), tile_at(rstd, b),
                                            ALU.subtract, ALU.mult).then_inc(normed_x, 1)
                    dve.wait_ge(full_d, ring_d.count(b, ("query", 1)))
                    for h in range(H // 2, H):
                        r, m = HD * (h % HG), h // HG
                        last = nc.vector.tensor_scalar(queries_t[r:r + HD, h, :], ring_d.bank(("query", 1))[r:r + HD, (m - 2) * P:(m - 1) * P],
                                                       bias[r:r + HD, 0, m:m + 1], SCALE, ALU.add, ALU.mult)
                    last.then_inc(out_d, 1)
                    for c in range(NCH):
                        key = ("key", c, LAST)
                        dve.wait_ge(full_d, ring_d.count(b, key))
                        nc.vector.tensor_scalar(keys_t[:, LAST, c * CH:(c + 1) * CH], ring_d.bank(key)[:],
                                                bias[:, 1, LAST:LAST + 1], None, ALU.add).then_inc(out_d, 1)
                        key = ("value", c, LAST)
                        dve.wait_ge(full_d, ring_d.count(b, key))
                        nc.vector.tensor_copy(values[:, 4 * c + LAST, :], ring_d.bank(key)[:]).then_inc(out_d, 1)

                    def evict_turned(h):
                        key = ("turned", h, LAST)
                        dve.wait_ge(full_d, ring_d.count(b, key))
                        nc.vector.tensor_copy(weights_t[:, 4 * LAST:4 * LAST + 4, (h % HG) * P:(h % HG + 1) * P],
                                              ring_d.bank(key)[:].rearrange("p (k q) -> p k q", q=P)).then_inc(out_d, 1)

                    def evict_heads(g):
                        dve.wait_ge(full_d, ring_d.count(b, ("heads", g)))
                        bank = ring_d.bank(("heads", g))
                        for r in range(HG):
                            rows = slice(r * HD, (r + 1) * HD)
                            last = nc.vector.tensor_scalar(heads_t[rows, g, :], bank[rows, r * P:(r + 1) * P],
                                                           bias[rows, 2, g:g + 1], None, ALU.add)
                        last.then_inc(out_d, 1)

                    for h in range(H):
                        e = h % 2
                        for c in range(NCH):
                            dve.wait_ge(scored, (b * H + h) * NCH + c + 1)
                            last = nc.vector.tensor_reduce(part_max[:, e, c:c + 1], score[:, c * CH:(c + 1) * CH], AX.X, ALU.max)
                        link(last)
                        nc.vector.tensor_reduce(neg_max[:, e:e + 1], part_max[:, e, :], AX.X, ALU.max, negate=True).then_inc(maxed, 1)
                        if h >= 1:
                            evict_turned(h - 1)
                        dve.wait_ge(exped, (b * H + h) * NCH + 2 * NCH)
                        link(nc.vector.tensor_reduce(total[:, e:e + 1], part_total[:, e, :], AX.X, ALU.add))
                        link(nc.vector.reciprocal(scale[:, e:e + 1], total[:, e:e + 1]))
                        for c in range(NCH):
                            cols = slice(c * CH, (c + 1) * CH)
                            nc.vector.tensor_scalar(weights[:, e, cols], weights[:, e, cols], scale[:, e:e + 1], None,
                                                    ALU.mult).then_inc(scaled, 1)
                        if h % HG == 0 and h:
                            evict_heads(h // HG - 1)
                    evict_turned(H - 1)
                    evict_heads(NG - 1)
                    xt = columns(x_sb, b)
                    link(nc.vector.tensor_tensor(xt, xt, bias_o[:], ALU.add))
                    for n in range(2):
                        key = ("output", n)
                        cols = slice(n * D // 2, (n + 1) * D // 2)
                        dve.wait_ge(full_d, ring_d.count(b, key))
                        nc.vector.tensor_tensor(xt[:, cols], xt[:, cols], ring_d.bank(key)[:, 0:D // 2], ALU.add).then_inc(out_d, 1)
                    dve.wait_ge(out_d, ring_d.landed(b, ("output", 1)))
                    link.close()

            @block.tensor
            def _(pe):
                with pe.Fori(0, B) as b:
                    def start(key):
                        r = ring(key)
                        pe.wait_ge(r.out, r.count(b, key))
                        return r.bank(key)

                    pe.wait_ge(normed_x, b + 1)
                    for n in range(2):
                        bank = start(("hidden", n))
                        for c in range(2):
                            last = nc.tensor.transpose(bank[:, c * P:(c + 1) * P],
                                                       hidden[:, (2 * n + c) * P:(2 * n + c + 1) * P], ident[:])
                        last.then_inc(ring(("hidden", n)).full, 1)
                    pe.wait_ge(w_loaded["q"], 16)
                    for n in range(2):
                        key = ("query", n)
                        if n == 0:
                            wait_tiles(pe, b, (ring_a, ring_d), key, ("hidden", 1))
                        else:
                            pe.wait_ge(out_d, ring_d.count(b, key))
                        bank = ring(key).bank(key)
                        for m in range(2):
                            for c in range(DC):
                                last = nc.tensor.matmul(bank[:, m * P:(m + 1) * P], w["q"][:, c, (2 * n + m) * P:(2 * n + m + 1) * P],
                                                        hidden_t[:, c, :], start=c == 0, stop=c == DC - 1)
                        last.then_inc(ring(key).full, 1)
                    for c in range(NCH):
                        pe.wait_ge(ctx_t_landed[c % 2], b * 32 + 16 * (c // 2) + 16)
                        pe.wait_ge(w_loaded["k"], 16)
                        for m in range(DC):
                            key = ("key", c, m)
                            bank = start(key)
                            for t in range(DC):
                                last = nc.tensor.matmul(bank[:], w["k"][:, t, m * P:(m + 1) * P], context_t[:, c % 2, t, :],
                                                        start=t == 0, stop=t == DC - 1)
                            last.then_inc(ring(key).full, 1)
                        pe.wait_ge(w_loaded["v"], 16)
                        for k in range(DC):
                            key = ("value", c, k)
                            bank = start(key)
                            for t in range(DC):
                                last = nc.tensor.matmul(bank[:], context_t[:, c % 2, t, k * P:(k + 1) * P], w["v"][:, t, :],
                                                        start=t == 0, stop=t == DC - 1)
                            last.then_inc(ring(key).full, 1)

                    def scores(h):
                        if h == 0:
                            pe.wait_ge(out_d, ring_d.landed(b, ("value", NCH - 1, DC - 1)))
                            pe.wait_ge(out_a, ring_a.landed(b, ("value", NCH - 1, DC - 2)))
                        for c in range(NCH):
                            pe.wait_ge(exped, (b * H + h) * NCH + c + 1)
                            nc.tensor.matmul(score[:, c * CH:(c + 1) * CH], queries_t[:, h, :],
                                             keys_t[:, h // HG, c * CH:(c + 1) * CH], start=True, stop=True).then_inc(scored, 1)

                    def turn(h):
                        for n in range(NCH):
                            key = ("turned", h, n)
                            pe.wait_ge(scaled, (b * H + h) * NCH + n + 1)
                            bank = start(key)
                            for k in range(4):
                                last = nc.tensor.transpose(bank[:, k * P:(k + 1) * P],
                                                           weights[:, h % 2, (4 * n + k) * P:(4 * n + k + 1) * P], ident[:])
                            last.then_inc(ring(key).full, 1)

                    def attend(g):
                        h = HG * g + HG - 1
                        wait_tiles(pe, b, (ring_a, ring_d), ("heads", g), ("turned", h, LAST))
                        for k in range(KT):
                            if k % 4 == 0 and k // 4 in BY_ACT:
                                pe.wait_ge(out_a, ring_a.landed(b, ("turned", h, k // 4)))
                            last = nc.tensor.matmul(ring_d.bank(("heads", g))[:], values[:, k, g * P:(g + 1) * P], weights_t[:, k, :],
                                                    start=k == 0, stop=k == KT - 1)
                        last.then_inc(full_d, 1)

                    for h in range(H):
                        scores(h)
                        if h >= 1:
                            turn(h - 1)
                        if h % HG == 0 and h:
                            attend(h // HG - 1)
                    turn(H - 1)
                    attend(NG - 1)
                    for n in range(2):
                        key = ("output", n)
                        cols = slice(n * D // 2, (n + 1) * D // 2)
                        wait_tiles(pe, b, (ring_a, ring_d), key, ("heads", NG - 1))
                        pe.wait_ge(w_loaded["o"], 16)
                        for g in range(NG):
                            last = nc.tensor.matmul(ring_d.bank(key)[:, 0:D // 2], heads_t[:, g, :], w["o"][:, g, cols],
                                                    start=g == 0, stop=g == NG - 1)
                        last.then_inc(full_d, 1)


def kernel_attention(nc, x_sb, ident, a):
    H, HD, M = 16, 32, 128
    PAIR = 2
    HG = P // HD
    NG = H // HG
    SCALE = 1.0 / math.sqrt(HD)
    EPS = 1e-6
    INV_SQRT_M = 1.0 / math.sqrt(M)
    W = HD + 1
    SLOTS = 4
    with ExitStack() as ctx:
        s = Space(nc, ctx, "features")
        w = {name: s.sb("w" + name, [P, DC, D]) for name in ("q", "k", "v", "o")}
        proj = s.sb("proj", [P, NG, HG, M])
        bias_o = s.sb("bias_o", [P, D])
        hidden = s.sb("hidden", [P, PAIR, D])
        hidden_t = s.sb("hidden_t", [P, PAIR, DC, P])
        side = s.sb("side", [P, PAIR, 2, D])
        side_t = s.sb("side_t", [P, PAIR, 2, DC, P])
        squares = s.sb("squares", [P, D])
        norms = s.sb("norms", [P, PAIR, 2, H])
        factor = s.sb("factor", [P, PAIR, 2, H])
        values = s.sb("values", [P, PAIR, H, W])
        exps = s.sb("exps", [P, SLOTS, HG, M])
        features = s.sb("features", [P, PAIR, 2, H, M])
        features_t = s.sb("features_t", [P, PAIR, H, P])
        sums = s.sb("sums", [P, PAIR, H, W])
        den = s.sb("den", [P, H])
        heads = s.sb("heads", [P, PAIR, D])
        heads_t = s.sb("heads_t", [P, PAIR, DC, P])
        stats, mv = s.sb("stats", [P, B, 6]), s.sb("mv", [P, B, 2])
        var, tmp, rstd, means = (s.sb(n, [P, B]) for n in ("var", "tmp", "rstd", "means"))
        neg_max = s.sb("neg_max", [P, SLOTS, HG])
        bank_a = [s.ps(f"bank_a{n}", [P, CH]) for n in range(2)]
        bank_d = [s.ps(f"bank_d{n}", [P, CH]) for n in range(2)]
        score = [s.ps(f"score{n}", [P, CH]) for n in range(SLOTS)]

        loaded = s.sem("loaded")
        w_loaded = {name: s.sem("loaded_" + name) for name in w}
        zeroed = s.sem("zeroed")
        ones_set = s.sem("ones_set")
        normed_x = s.sem("normed_x")
        full_a, out_a = s.sem("full_a"), s.sem("out_a")
        full_d, out_d = s.sem("full_d"), s.sem("out_d")
        scored, maxed, exped, featured = s.sem("scored"), s.sem("maxed"), s.sem("exped"), s.sem("featured")
        squared, factored = s.sem("squared"), s.sem("factored")
        chain, chain_ln = s.sem("chain"), s.sem("chain_ln")

        QUERY, KEY = 0, 1

        def front(j):
            out = [("hidden", j, 0)]
            out += [("side", j, QUERY), ("side", j, KEY), ("value", j, 0), ("square", j, QUERY), ("square", j, KEY)]
            return out + [("side_t", j, QUERY), ("side_t", j, KEY)]

        def score_steps(j):
            names = [(q, g) for q in (KEY, QUERY) for g in range(NG)]
            out = []
            for n, (q, g) in enumerate(names):
                out += [("score", j, q * NG + g)] + ([("feature", j, names[n - 1][0] * NG + names[n - 1][1])] if n else [])
            return out + [("feature", j, QUERY * NG + NG - 1)]

        def back(j):
            out = [("sums", j, 0), ("sums", j, 1)] + [("features_t", j, g) for g in range(NG)]
            return out + [("heads", j, 0), ("heads", j, 1), ("heads_t", j, 0), ("output", j, 0)]

        steps = front(0) + merged(score_steps(0), front(1)) + merged(score_steps(1), back(0)) + back(1)
        ON_SCALAR = {("side", QUERY), ("value", 0), ("side_t", QUERY), ("side_t", KEY), ("features_t", 0), ("features_t", 2),
                     ("sums", 0), ("heads_t", 0)}
        tiles = [t for t in steps if t[0] not in ("score", "feature", "square")]
        ring_a = Ring(bank_a, full_a, out_a, [t for t in tiles if (t[0], t[2]) in ON_SCALAR])
        ring_d = Ring(bank_d, full_d, out_d, [t for t in tiles if (t[0], t[2]) not in ON_SCALAR])
        SCORES = PAIR * 2 * NG
        order_of = {t[1:]: k for k, t in enumerate([t for t in steps if t[0] == "score"])}
        LINKS = PAIR * (2 * 2 + 2 * 2 + 1)
        LOADS = 1 + H

        with nc.Block() as block:

            @block.sync
            def _(sp):
                for name in w:
                    load(sp, w[name][:], a["w" + name], w_loaded[name])
                sp.dma_start(bias_o[:], broadcast(a["bo"])).then_inc(loaded, 16)
                sp.wait_ge(zeroed, 1)
                for h in range(H):
                    r = h % HG
                    sp.dma_start(proj[r * HD:(r + 1) * HD, h // HG, r, :], a["proj"][h]).then_inc(loaded, 16)

            @block.gpsimd
            def _(pool):
                nc.gpsimd.memset(proj[:], 0.0).then_inc(zeroed, 1)
                nc.gpsimd.memset(values[:], 1.0).then_inc(ones_set, 1)

            @block.scalar
            def _(act):
                act.sem_inc(out_a, 2)
                act.sem_inc(exped, SLOTS)
                act.wait_ge(ones_set, 1)
                with act.Fori(0, B // PAIR) as i:
                    for t in steps:
                        what, j, n = t
                        if what == "score":
                            k = order_of[t[1:]]
                            e = k % SLOTS
                            act.wait_ge(maxed, i * SCORES + k + 1)
                            act.wait_ge(featured, i * SCORES + k + 1)
                            for r in range(HG):
                                last = nc.scalar.activation(exps[:, e, r, :], score[e][:, r * M:(r + 1) * M], ACT.Exp,
                                                            bias=neg_max[:, e, r:r + 1])
                            last.then_inc(exped, 1)
                        elif what == "square":
                            act.wait_ge(squared, i * 2 * PAIR + 2 * j + n + 1)
                            nc.scalar.activation(factor[:, j, n, :], norms[:, j, n, :], ACT.Exp, scale=-0.5).then_inc(factored, 1)
                        elif t in ring_a.at:
                            act.wait_ge(full_a, ring_a.count(i, t))
                            bank = ring_a.bank(t)
                            if what == "side":
                                last = nc.scalar.mul(side[:, j, n, :], bank[:], SCALE)
                            elif what == "value":
                                last = nc.scalar.copy(values[:, j, :, 0:HD], bank[:].rearrange("p (h d) -> p h d", d=HD))
                            elif what == "side_t":
                                last = nc.scalar.copy(side_t[:, j, n], bank[:].rearrange("p (c q) -> p c q", q=P))
                            elif what == "features_t":
                                last = nc.scalar.copy(features_t[:, j, HG * n:HG * n + HG, :], bank[:].rearrange("p (h q) -> p h q", q=P))
                            elif what == "sums":
                                last = nc.scalar.copy(sums[:, j, 8 * n:8 * n + 8, :], bank[:, 0:8 * W].rearrange("p (h w) -> p h w", w=W))
                            elif what == "heads_t":
                                last = nc.scalar.copy(heads_t[:, j], bank[:].rearrange("p (c q) -> p c q", q=P))
                            last.then_inc(out_a, 1)

            @block.vector
            def _(dve):
                dve.sem_inc(out_d, 2)
                dve.sem_inc(featured, SLOTS)
                first = Chain(dve, chain_ln)
                tile_stats(nc, first, x_sb, stats, mv, tmp[:], rstd[:], var[:])
                first(nc.vector.tensor_copy(means[:], mv[:, :, 0]))
                dve.wait_ge(loaded, 16 * LOADS)
                with dve.Fori(0, B // PAIR) as i:
                    link = Chain(dve, chain, LINKS, i)
                    for j in range(PAIR):
                        b = i * PAIR + j
                        nc.vector.tensor_scalar(hidden[:, j, :], columns(x_sb, b), tile_at(means, b), tile_at(rstd, b),
                                                ALU.subtract, ALU.mult).then_inc(normed_x, 1)
                    for t in steps:
                        what, j, n = t
                        if what == "score":
                            k = order_of[t[1:]]
                            e = k % SLOTS
                            dve.wait_ge(scored, i * SCORES + k + 1)
                            nc.vector.tensor_reduce(neg_max[:, e, :], score[e][:].rearrange("p (r m) -> p r m", m=M),
                                                    AX.X, ALU.max, negate=True).then_inc(maxed, 1)
                        elif what == "feature":
                            k = order_of[t[1:]]
                            e, q, g = k % SLOTS, n // NG, n % NG
                            dve.wait_ge(exped, i * SCORES + k + 1 + SLOTS)
                            for r in range(HG):
                                h = HG * g + r
                                last = nc.vector.tensor_scalar(features[:, j, q, h, :], exps[:, e, r, :], factor[:, j, q, h:h + 1],
                                                               EPS * INV_SQRT_M, ALU.mult, ALU.add)
                            last.then_inc(featured, 1)
                        elif what == "square":
                            if n == QUERY:
                                dve.wait_ge(out_a, ring_a.landed(i, ("side", j, n)))
                            else:
                                dve.wait_ge(out_d, ring_d.landed(i, ("side", j, n)))
                            link(nc.vector.tensor_tensor(squares[:], side[:, j, n, :], side[:, j, n, :], ALU.mult))
                            nc.vector.tensor_reduce(norms[:, j, n, :], squares[:].rearrange("p (h d) -> p h d", d=HD),
                                                    AX.X, ALU.add).then_inc(squared, 1)
                            dve.wait_ge(factored, i * 2 * PAIR + 2 * j + n + 1)
                            link(nc.vector.tensor_scalar(factor[:, j, n, :], factor[:, j, n, :], INV_SQRT_M, None, ALU.mult))
                        elif t in ring_d.at:
                            dve.wait_ge(full_d, ring_d.count(i, t))
                            bank = ring_d.bank(t)
                            if what == "hidden":
                                last = nc.vector.tensor_copy(hidden_t[:, j], bank[:].rearrange("p (c q) -> p c q", q=P))
                            elif what == "side":
                                last = nc.vector.tensor_scalar(side[:, j, n, :], bank[:], SCALE, None, ALU.mult)
                            elif what == "features_t":
                                last = nc.vector.tensor_copy(features_t[:, j, HG * n:HG * n + HG, :], bank[:].rearrange("p (h q) -> p h q", q=P))
                            elif what == "sums":
                                last = nc.vector.tensor_copy(sums[:, j, 8 * n:8 * n + 8, :], bank[:, 0:8 * W].rearrange("p (h w) -> p h w", w=W))
                            elif what == "heads":
                                view = bank[:, 0:8 * W].rearrange("p (h w) -> p h w", w=W)
                                link(nc.vector.tensor_scalar(den[:, 8 * n:8 * n + 8], view[:, :, HD], EPS, None, ALU.add))
                                link(nc.vector.reciprocal(den[:, 8 * n:8 * n + 8], den[:, 8 * n:8 * n + 8]))
                                last = nc.vector.tensor_tensor(heads[:, j, 8 * n * HD:8 * (n + 1) * HD].rearrange("p (h d) -> p h d", d=HD),
                                                               view[:, :, 0:HD], den[:, 8 * n:8 * n + 8].unsqueeze(2).broadcast_to([P, 8, HD]), ALU.mult)
                            elif what == "output":
                                xt = columns(x_sb, i * PAIR + j)
                                link(nc.vector.tensor_tensor(xt, xt, bank[:], ALU.add))
                                last = nc.vector.tensor_tensor(xt, xt, bias_o[:], ALU.add)
                            last.then_inc(out_d, 1)
                    link.close()

            @block.tensor
            def _(pe):
                with pe.Fori(0, B // PAIR) as i:
                    rings = (ring_a, ring_d)
                    for t in steps:
                        what, j, n = t
                        if what in ("feature", "square"):
                            continue
                        if what == "score":
                            k = order_of[t[1:]]
                            q, g = n // NG, n % NG
                            pe.wait_ge(out_a, ring_a.landed(i, ("side_t", j, q)))
                            pe.wait_ge(loaded, 16 * LOADS)
                            pe.wait_ge(exped, i * SCORES + k + 1)
                            nc.tensor.matmul(score[k % SLOTS][:], side_t[:, j, q, g, :], proj[:, g].rearrange("p r m -> p (r m)"),
                                             start=True, stop=True).then_inc(scored, 1)
                            continue
                        reads = {"side": [("hidden", j, 0)], "value": [("hidden", j, 0)], "side_t": [("side", j, n)],
                                 "sums": [("value", j, 0)], "heads": [("sums", j, n)] + [("features_t", j, g) for g in (2 * n, 2 * n + 1)],
                                 "heads_t": [("heads", j, 0), ("heads", j, 1)], "output": [("heads_t", j, 0)]}
                        wait_tiles(pe, i, rings, t, *reads.get(what, []))
                        r = ring_a if t in ring_a.at else ring_d
                        bank = r.bank(t)
                        if what == "hidden":
                            pe.wait_ge(normed_x, i * PAIR + j + 1)
                            for c in range(DC):
                                last = nc.tensor.transpose(bank[:, c * P:(c + 1) * P], hidden[:, j, c * P:(c + 1) * P], ident[:])
                        elif what in ("side", "value"):
                            name = "v" if what == "value" else "qk"[n]
                            pe.wait_ge(w_loaded[name], 16)
                            for c in range(DC):
                                last = nc.tensor.matmul(bank[:], hidden_t[:, j, c, :], w[name][:, c, :], start=c == 0, stop=c == DC - 1)
                        elif what == "side_t":
                            for c in range(DC):
                                last = nc.tensor.transpose(bank[:, c * P:(c + 1) * P], side[:, j, n, c * P:(c + 1) * P], ident[:])
                        elif what == "sums":
                            pe.wait_ge(featured, i * SCORES + order_of[(j, KEY * NG + 2 * n + 1)] + 1 + SLOTS)
                            for h in range(8):
                                last = nc.tensor.matmul(bank[:, h * W:(h + 1) * W], features[:, j, KEY, 8 * n + h, :],
                                                        values[:, j, 8 * n + h, :], start=True, stop=True)
                        elif what == "features_t":
                            pe.wait_ge(featured, i * SCORES + order_of[(j, QUERY * NG + n)] + 1 + SLOTS)
                            for h in range(HG):
                                last = nc.tensor.transpose(bank[:, h * P:(h + 1) * P], features[:, j, QUERY, HG * n + h, :], ident[:])
                        elif what == "heads":
                            for h in range(8):
                                last = nc.tensor.matmul(bank[:, h * W:(h + 1) * W], features_t[:, j, 8 * n + h, :],
                                                        sums[:, j, 8 * n + h, :], start=True, stop=True)
                        elif what == "heads_t":
                            for c in range(DC):
                                last = nc.tensor.transpose(bank[:, c * P:(c + 1) * P], heads[:, j, c * P:(c + 1) * P], ident[:])
                        elif what == "output":
                            pe.wait_ge(w_loaded["o"], 16)
                            for c in range(DC):
                                last = nc.tensor.matmul(bank[:], heads_t[:, j, c, :], w["o"][:, c, :], start=c == 0, stop=c == DC - 1)
                        last.then_inc(r.full, 1)


def scalar_nets(nc, x_sb, out_dram, ident, a):
    M, INNER = 64, 16
    TURNS = 2
    NB = B // TURNS
    UNITS = INNER // 2
    with ExitStack() as ctx:
        s = Space(nc, ctx, "nets")
        w_in = s.sb("w_in", [P, DC, P])
        bias_in = s.sb("bias_in", [P, 1])
        w1, b1, w2 = (s.sb(n, [P, UNITS]) for n in ("w1", "b1", "w2"))
        b2 = s.sb("b2", [P, 1])
        w_out = s.sb("w_out", [P, D])
        bias_out = s.sb("bias_out", [P, D])
        hidden = s.sb("hidden", [P, B, D])
        hidden_t = s.sb("hidden_t", [P, DC, NB * P])
        scalars = s.sb("scalars", [P, NB * P])
        units = s.sb("units", [P, UNITS, NB * P])
        sums = s.sb("sums", [P, 2, NB * P])
        stats, mv = s.sb("stats", [P, B, 6]), s.sb("mv", [P, B, 2])
        var, tmp, rstd = (s.sb(n, [P, B]) for n in ("var", "tmp", "rstd"))
        bank_a = [s.ps(f"bank_a{n}", [P, CH]) for n in range(2)]
        bank_d = [s.ps(f"bank_d{n}", [P, CH]) for n in range(4)]
        bank_s = s.ps("bank_s", [P, NB * P])
        full_s = s.sem("full_s")
        loaded, normed_x, zeroed = s.sem("loaded"), s.sem("normed_x"), s.sem("zeroed")
        full_a, out_a = s.sem("full_a"), s.sem("out_a")
        full_d, out_d = s.sem("full_d"), s.sem("out_d")
        relued, summed, stored = s.sem("relued"), s.sem("summed"), s.sem("stored")
        chain = s.sem("chain")
        ring_a = Ring(bank_a, full_a, out_a, [("token", n) for n in range(NB)])
        ring_d = Ring(bank_d, full_d, out_d, [("output", n) for n in range(NB)])
        LOADS = 2 * 6 + 2

        with nc.Block() as block:

            @block.sync
            def _(sp):
                sp.wait_ge(zeroed, 1)
                for half in range(2):
                    rows = slice(half * M, (half + 1) * M)
                    units_of = slice(half * UNITS, (half + 1) * UNITS)
                    sp.dma_start(w_in[:, :, rows], a["Win"].rearrange("(c p) m -> p c m", p=P)).then_inc(loaded, 16)
                    sp.dma_start(bias_in[rows, :], a["bin"].unsqueeze(1)).then_inc(loaded, 16)
                    for dst, name in ((w1, "W1"), (b1, "b1"), (w2, "W2")):
                        sp.dma_start(dst[rows, :], a[name][:, units_of]).then_inc(loaded, 16)
                    sp.dma_start(w_out[rows, :], a["Wout"]).then_inc(loaded, 16)
                sp.dma_start(b2[0:M, :], a["b2"].unsqueeze(1)).then_inc(loaded, 16)
                sp.dma_start(bias_out[:], broadcast(a["bout"])).then_inc(loaded, 16)
                for i in range(TURNS):
                    sp.wait_ge(out_d, ring_d.landed(i, ("output", NB - 1)))
                    sp.dma_start(out_dram[i * NB:(i + 1) * NB].rearrange("b p d -> p b d"), x_sb[:, i * NB:(i + 1) * NB, :]).then_inc(stored, 16)
                sp.wait_ge(stored, 16 * TURNS)

            @block.gpsimd
            def _(pool):
                nc.gpsimd.memset(b2[:], 0.0).then_inc(zeroed, 1)

            @block.scalar
            def _(act):
                act.sem_inc(out_a, 2)
                act.wait_ge(loaded, 16 * LOADS)
                for i in range(TURNS):
                    for n in range(NB):
                        t = ("token", n)
                        act.wait_ge(full_a, ring_a.count(i, t))
                        nc.scalar.copy(hidden_t[:, :, n * P:(n + 1) * P], ring_a.bank(t)[:].rearrange("p (c q) -> p c q", q=P)).then_inc(out_a, 1)
                    act.wait_ge(summed, i * (UNITS + 1) + 1)
                    for u in range(UNITS):
                        nc.scalar.activation(units[:, u, :], scalars[:], ACT.Relu, bias=b1[:, u:u + 1], scale=w1[:, u:u + 1]).then_inc(relued, 1)

            @block.vector
            def _(dve):
                dve.sem_inc(out_d, 4)
                link = Chain(dve, chain)
                tile_stats(nc, link, x_sb, stats, mv, tmp[:], rstd[:], var[:])
                for b in range(B):
                    nc.vector.tensor_scalar(hidden[:, b, :], x_sb[:, b, :], mv[:, b, 0:1], rstd[:, b:b + 1],
                                            ALU.subtract, ALU.mult).then_inc(normed_x, 1)
                dve.wait_ge(loaded, 16 * LOADS)
                for i in range(TURNS):
                    dve.wait_ge(full_s, i + 1)
                    nc.vector.tensor_scalar(scalars[:], bank_s[:], bias_in[:], None, ALU.add).then_inc(summed, 1)
                    for u in range(UNITS):
                        dve.wait_ge(relued, i * UNITS + u + 1)
                        if u == 0:
                            last = nc.vector.tensor_scalar(sums[:, u % 2, :], units[:, u, :], w2[:, u:u + 1], b2[:], ALU.mult, ALU.add)
                        else:
                            dve.wait_ge(summed, i * (UNITS + 1) + u + 1)
                            last = nc.vector.scalar_tensor_tensor(out=sums[:, u % 2, :], in0=units[:, u, :], scalar=w2[:, u:u + 1],
                                                                  in1=sums[:, (u - 1) % 2, :], op0=ALU.mult, op1=ALU.add)
                        last.then_inc(summed, 1)
                    for n in range(NB):
                        t = ("output", n)
                        dve.wait_ge(full_d, ring_d.count(i, t))
                        xt = x_sb[:, i * NB + n, :]
                        link(nc.vector.tensor_tensor(xt, xt, ring_d.bank(t)[:], ALU.add))
                        nc.vector.tensor_tensor(xt, xt, bias_out[:], ALU.add).then_inc(out_d, 1)

            @block.tensor
            def _(pe):
                pe.wait_ge(loaded, 16 * LOADS)
                for i in range(TURNS):
                    for n in range(NB):
                        t = ("token", n)
                        pe.wait_ge(out_a, ring_a.count(i, t))
                        pe.wait_ge(normed_x, i * NB + n + 1)
                        for c in range(DC):
                            last = nc.tensor.transpose(ring_a.bank(t)[:, c * P:(c + 1) * P], hidden[:, i * NB + n, c * P:(c + 1) * P], ident[:])
                        last.then_inc(full_a, 1)
                    pe.wait_ge(out_a, ring_a.landed(i, ("token", NB - 1)))
                    for c in range(DC):
                        last = nc.tensor.matmul(bank_s[:], w_in[:, c, :], hidden_t[:, c, :], start=c == 0, stop=c == DC - 1)
                    last.then_inc(full_s, 1)
                    pe.wait_ge(summed, (i + 1) * (UNITS + 1))
                    for n in range(NB):
                        t = ("output", n)
                        pe.wait_ge(out_d, ring_d.count(i, t))
                        nc.tensor.matmul(ring_d.bank(t)[:], sums[:, (UNITS - 1) % 2, n * P:(n + 1) * P], w_out[:],
                                         start=True, stop=True).then_inc(full_d, 1)


def perceiver(nc, t, out):
    vs_dram = nc.dram_tensor("attended_context", (2 * B, D, CH), F32, kind="Internal").ap()
    with ExitStack() as ctx:
        s = Space(nc, ctx, "whole")
        x_sb = s.sb("x", [P, B, D])
        ident = s.sb("ident", [P, P])
        ready = s.sem("ready")
        with nc.Block() as block:

            @block.sync
            def _(sp):
                sp.dma_start(ident[:], t["identity"]).then_inc(ready, 16)
                sp.wait_ge(ready, 16)

        swishmax_context(nc, t["x"], x_sb, ident, t["context"], t["context_t"],
                         {"key_down": t["L0_xattn_key_down"], "query_down": t["L0_xattn_query_down"],
                          "query_bias": t["L0_xattn_query_down_bias"]}, vs_dram)
        swishmax_output(nc, x_sb, {"value_down": t["L0_xattn_value_down"], "value_up": t["L0_xattn_value_up"]}, vs_dram)
        part = {n: t["L0_attn_" + n] for n in ("gamma", "beta", "lambda_q1", "lambda_k1", "lambda_q2", "lambda_k2")}
        part |= {"w" + n: t["L0_attn_W" + n] for n in "qkvo"}
        token_attention(nc, "twin", x_sb, ident, part, True, "norm")
        with ExitStack() as inner:
            mid = Space(nc, inner, "layer0").sb("mid", [P, B, D])
            norm_tiles(nc, x_sb, mid)
            part = {"g": t["L0_ffn_g1"], "b": t["L0_ffn_b1"]}
            part |= {"w" + n: t["L0_ffn_W" + n] for n in "qkvo"}
            token_attention(nc, "plain", mid, ident, part, False, "add")
            experts(nc, x_sb, mid, ident, {"g2": t["L0_ffn_g2"], "b2": t["L0_ffn_b2"], "Wg": t["L0_ffn_Wg"],
                                           "W1": t["L0_ffn_W1"], "W2": t["L0_ffn_W2"], "numbers": t["numbers"]})
        part = {"w" + n: t["L1_xattn_W" + n] for n in "qkvo"} | {"b" + n: t["L1_xattn_b" + n] for n in "qkvo"}
        softmax_context(nc, x_sb, ident, t["context_t"], part)
        part = {"w" + n: t["L1_attn_W" + n] for n in "qkvo"} | {"bo": t["L1_attn_bo"], "proj": t["L1_attn_proj"]}
        kernel_attention(nc, x_sb, ident, part)
        scalar_nets(nc, x_sb, out, ident, {"Win": t["L1_ffn_Win"], "bin": t["L1_ffn_bin_"], "W1": t["L1_ffn_W1"],
                                           "b1": t["L1_ffn_b1"], "W2": t["L1_ffn_W2"], "b2": t["L1_ffn_b2"],
                                           "Wout": t["L1_ffn_Wout"], "bout": t["L1_ffn_bout"]})


def _layout(inputs):
    import numpy as np

    a = {k: np.asarray(v) for k, v in inputs.items()}
    context = a.pop("ctx_1024")
    chunks = context.reshape(B, NCH, CH, D)
    a["context"] = chunks.reshape(B * NCH, CH, D)
    a["context_t"] = chunks.transpose(0, 1, 3, 2).reshape(B * NCH, D, CH)
    for name in ("L0_xattn_key_down", "L0_xattn_query_down"):
        a[name] = a[name].transpose(1, 0, 2).reshape(D, D)
    a["L0_xattn_query_down_bias"] = a["L0_xattn_query_down_bias"].reshape(DC, P).T
    for n in "qkv":
        a["L1_xattn_b" + n] = a["L1_xattn_b" + n].reshape(DC, P).T
    for layer in ("L1_xattn_W", "L1_attn_W"):
        for n in "qkvo":
            a[layer + n] = a[layer + n].T
    a["L1_attn_proj"] = a["L1_attn_proj"].transpose(0, 2, 1)
    a["identity"] = np.eye(P, dtype=np.float32)
    a["numbers"] = np.arange(8, dtype=np.float32)
    return {k: np.ascontiguousarray(v) for k, v in a.items()}


def kernel(**inputs):
    import concourse.bacc as bacc
    from concourse.bass_utils import run_bass_kernel_spmd

    nc = bacc.Bacc("TRN2", target_bir_lowering=False, num_devices=1)
    arrays = _layout(inputs)
    drams = {k: nc.dram_tensor(f"in_{k}_dram", v.shape, mybir.dt.from_np(v.dtype), kind="ExternalInput").ap()
             for k, v in arrays.items()}
    out = nc.dram_tensor("out_0_dram", (B, P, D), F32, kind="ExternalOutput").ap()
    perceiver(nc, drams, out)
    r = run_bass_kernel_spmd(nc, [{f"in_{k}_dram": v for k, v in arrays.items()}], core_ids=[0])
    return r.results[0]["out_0_dram"]
```
